# Optimizing a Trainium2 kernel written in Bass

```python
import numpy as np
import jax
import jax.numpy as jnp

def _softmax(x, axis=-1):
    return jax.nn.softmax(x, axis=axis)

def _gelu(x):
    return jax.nn.gelu(x, approximate=True)

def _silu(x):
    return jax.nn.silu(x)

def _sigmoid(x):
    return jax.nn.sigmoid(x)

def _layernorm(x, axis=-1, eps=1e-05):
    m = jnp.mean(x, axis=axis, keepdims=True)
    v = jnp.var(x, axis=axis, keepdims=True)
    return (x - m) / jnp.sqrt(v + eps)

def _scatter_add(tgt, idx, src, axis=0):
    return tgt.at[idx].add(src)

def _segment_sum(src, seg, n):
    return jax.ops.segment_sum(src, seg, n)
kernel_name = 'mk_hybrid_d1_jaxref_r8_ee8180'

def setup_inputs(seed: int=0):
    np.random.seed(seed)
    _w = jnp.asarray

    def _L0_attn_a_setup():
        import jax, jax.numpy as jnp
        import numpy as np
        HEADS = 16

        def _binarize(W):
            alpha = jnp.mean(jnp.abs(W), axis=tuple(range(1, W.ndim)), keepdims=True)
            B = W + jax.lax.stop_gradient(jnp.sign(W) - W)
            return alpha * B

        def _binlinear(x, W, b):
            Wb = _binarize(W)
            return jnp.einsum('btc,oc->bto', x, Wb) + b
        key = jax.random.key(seed)
        ks = jax.random.split(key, 9)
        dim = 128
        B, T = (4, 256)
        inp = {'x': jax.random.normal(ks[0], (B, T, dim), jnp.float32), 'Wq': jax.random.normal(ks[1], (dim, dim), jnp.float32) * 0.02, 'bq': jax.random.normal(ks[2], (dim,), jnp.float32) * 0.02, 'Wk': jax.random.normal(ks[3], (dim, dim), jnp.float32) * 0.02, 'bk': jax.random.normal(ks[4], (dim,), jnp.float32) * 0.02, 'Wv': jax.random.normal(ks[5], (dim, dim), jnp.float32) * 0.02, 'bv': jax.random.normal(ks[6], (dim,), jnp.float32) * 0.02, 'Wp': jax.random.normal(ks[7], (dim, dim), jnp.float32) * 0.02, 'bp': jax.random.normal(ks[8], (dim,), jnp.float32) * 0.02}
        return inp
    _L0_attn_a_in = _L0_attn_a_setup()

    def _L0_attn_b_setup():
        import jax, jax.numpy as jnp
        import numpy as np
        import math
        NUM_HEADS = 16
        MAX_REL_POS = 128
        key = jax.random.key(seed)
        ks = jax.random.split(key, 6)
        B, S, H = (4, 128, 128)
        hd = H // NUM_HEADS
        sc = 1.0 / math.sqrt(H)
        return {'x': jax.random.normal(ks[0], (B, S, H), jnp.float32), 'Wq': jax.random.normal(ks[1], (H, H), jnp.float32) * sc, 'bq': jnp.zeros((H,), jnp.float32), 'Wk': jax.random.normal(ks[2], (H, H), jnp.float32) * sc, 'bk': jnp.zeros((H,), jnp.float32), 'Wv': jax.random.normal(ks[3], (H, H), jnp.float32) * sc, 'bv': jnp.zeros((H,), jnp.float32), 'Wo': jax.random.normal(ks[4], (H, H), jnp.float32) * sc, 'bo': jnp.zeros((H,), jnp.float32), 'rel_emb': jax.random.normal(ks[5], (2 * MAX_REL_POS + 1, hd), jnp.float32) * 0.02}
    _L0_attn_b_in = _L0_attn_b_setup()

    def _L0_ffn_setup():
        import jax, jax.numpy as jnp
        import numpy as np
        B, L, D = (4, 128, 128)
        E, H = (8, 512)
        CAPACITY = 6
        key = jax.random.key(seed)
        ks = jax.random.split(key, 6)
        x = jax.random.normal(ks[0], (B, L, D), dtype=jnp.float32)
        gate_weight = jax.random.normal(ks[1], (E, D), dtype=jnp.float32) * 0.006
        w1 = jax.random.normal(ks[2], (E, H, D), dtype=jnp.float32) * 0.02
        b1 = jnp.zeros((E, H), dtype=jnp.float32)
        w2 = jax.random.normal(ks[3], (E, D, H), dtype=jnp.float32) * 0.02
        b2 = jnp.zeros((E, D), dtype=jnp.float32)
        return {'x': x, 'gate_weight': gate_weight, 'w1': w1, 'b1': b1, 'w2': w2, 'b2': b2}
    _L0_ffn_in = _L0_ffn_setup()
    _d = {'L0_attn_a_x': _L0_attn_a_in['x'], 'L0_attn_a_Wq': _L0_attn_a_in['Wq'], 'L0_attn_a_bq': _L0_attn_a_in['bq'], 'L0_attn_a_Wk': _L0_attn_a_in['Wk'], 'L0_attn_a_bk': _L0_attn_a_in['bk'], 'L0_attn_a_Wv': _L0_attn_a_in['Wv'], 'L0_attn_a_bv': _L0_attn_a_in['bv'], 'L0_attn_a_Wp': _L0_attn_a_in['Wp'], 'L0_attn_a_bp': _L0_attn_a_in['bp'], 'L0_attn_b_Wq': _L0_attn_b_in['Wq'], 'L0_attn_b_bq': _L0_attn_b_in['bq'], 'L0_attn_b_Wk': _L0_attn_b_in['Wk'], 'L0_attn_b_bk': _L0_attn_b_in['bk'], 'L0_attn_b_Wv': _L0_attn_b_in['Wv'], 'L0_attn_b_bv': _L0_attn_b_in['bv'], 'L0_attn_b_Wo': _L0_attn_b_in['Wo'], 'L0_attn_b_bo': _L0_attn_b_in['bo'], 'L0_attn_b_rel_emb': _L0_attn_b_in['rel_emb'], 'L0_ffn_gate_weight': _L0_ffn_in['gate_weight'], 'L0_ffn_w1': _L0_ffn_in['w1'], 'L0_ffn_b1': _L0_ffn_in['b1'], 'L0_ffn_w2': _L0_ffn_in['w2'], 'L0_ffn_b2': _L0_ffn_in['b2']}
    _x0 = _d['L0_attn_a_x']
    _d['L0_attn_a_x'] = jax.random.normal(jax.random.fold_in(jax.random.key(seed), 1), (16, 256, 128), dtype=_x0.dtype)
    del _x0
    return _d

def reference(L0_attn_a_x, L0_attn_a_Wq, L0_attn_a_bq, L0_attn_a_Wk, L0_attn_a_bk, L0_attn_a_Wv, L0_attn_a_bv, L0_attn_a_Wp, L0_attn_a_bp, L0_attn_b_Wq, L0_attn_b_bq, L0_attn_b_Wk, L0_attn_b_bk, L0_attn_b_Wv, L0_attn_b_bv, L0_attn_b_Wo, L0_attn_b_bo, L0_attn_b_rel_emb, L0_ffn_gate_weight, L0_ffn_w1, L0_ffn_b1, L0_ffn_w2, L0_ffn_b2):

    def _L0_attn_a_ref(x, Wq, bq, Wk, bk, Wv, bv, Wp, bp):
        import jax, jax.numpy as jnp
        import numpy as np
        HEADS = 16

        def _binarize(W):
            alpha = jnp.mean(jnp.abs(W), axis=tuple(range(1, W.ndim)), keepdims=True)
            B = W + jax.lax.stop_gradient(jnp.sign(W) - W)
            return alpha * B

        def _binlinear(x, W, b):
            Wb = _binarize(W)
            return jnp.einsum('btc,oc->bto', x, Wb) + b
        B, T, C = x.shape
        H = HEADS
        Dh = C // H
        scale = Dh ** (-0.5)

        def split_heads(t):
            return t.reshape(B, T, H, Dh).transpose(0, 2, 1, 3)
        q = split_heads(_binlinear(x, Wq, bq))
        k = split_heads(_binlinear(x, Wk, bk))
        v = split_heads(_binlinear(x, Wv, bv))
        att = jnp.einsum('bhtd,bhsd->bhts', q, k) * scale
        att = jax.nn.softmax(att, axis=-1)
        y = jnp.einsum('bhts,bhsd->bhtd', att, v)
        y = y.transpose(0, 2, 1, 3).reshape(B, T, C)
        return _binlinear(y, Wp, bp)

    def _L0_attn_b_ref(x, Wq, bq, Wk, bk, Wv, bv, Wo, bo, rel_emb):
        import jax, jax.numpy as jnp
        import numpy as np
        import math
        NUM_HEADS = 16
        MAX_REL_POS = 128
        B, S, H = x.shape
        nh = NUM_HEADS
        hd = H // nh
        inv_sqrt_d = 1.0 / math.sqrt(hd)

        def proj(W, b):
            return (x @ W.T + b).reshape(B, S, nh, hd).transpose(0, 2, 1, 3)
        Q = proj(Wq, bq)
        K = proj(Wk, bk)
        V = proj(Wv, bv)
        pos = jnp.arange(S)
        rel_idx = jnp.clip(pos[None, :] - pos[:, None], -MAX_REL_POS, MAX_REL_POS) + MAX_REL_POS
        E = rel_emb[rel_idx]
        scores = (jnp.einsum('bnqd,bnkd->bnqk', Q, K) + jnp.einsum('bnqd,qkd->bnqk', Q, E)) * inv_sqrt_d
        attn = jax.nn.softmax(scores, axis=-1)
        out = jnp.einsum('bnqk,bnkd->bnqd', attn, V)
        out = out.transpose(0, 2, 1, 3).reshape(B, S, H)
        return out @ Wo.T + bo

    def _L0_ffn_ref(x, gate_weight, w1, b1, w2, b2):
        import jax, jax.numpy as jnp
        import numpy as np
        B, L, D = (4, 128, 128)
        E, H = (8, 512)
        CAPACITY = 6
        logits = jnp.einsum('bld,ed->ble', x, gate_weight)
        expert_k = B * L * CAPACITY
        kth_val = jnp.sort(logits.reshape(-1))[expert_k - 1]
        mask = (logits >= kth_val).astype(x.dtype)
        gates = logits * mask
        h = jax.nn.gelu(jnp.einsum('bld,ehd->bleh', x, w1) + b1, approximate=True)
        y = jnp.einsum('bleh,edh->blde', h, w2) + b2.T[None, None]
        out = jnp.einsum('blde,ble->bld', y, gates)
        return out
    x = L0_attn_a_x
    x = x + _L0_attn_a_ref(_layernorm(x, axis=-1), L0_attn_a_Wq, L0_attn_a_bq, L0_attn_a_Wk, L0_attn_a_bk, L0_attn_a_Wv, L0_attn_a_bv, L0_attn_a_Wp, L0_attn_a_bp)
    x = x + _L0_ffn_ref(_layernorm(x, axis=-1), L0_ffn_gate_weight, L0_ffn_w1, L0_ffn_b1, L0_ffn_w2, L0_ffn_b2)
    x = x + _L0_attn_b_ref(_layernorm(x, axis=-1), L0_attn_b_Wq, L0_attn_b_bq, L0_attn_b_Wk, L0_attn_b_bk, L0_attn_b_Wv, L0_attn_b_bv, L0_attn_b_Wo, L0_attn_b_bo, L0_attn_b_rel_emb)
    x = x + _L0_ffn_ref(_layernorm(x, axis=-1), L0_ffn_gate_weight, L0_ffn_w1, L0_ffn_b1, L0_ffn_w2, L0_ffn_b2)
    return x

_drawn_inputs = setup_inputs


def setup_inputs(seed=0):
    import zlib

    import numpy as np

    out = dict(_drawn_inputs(seed))
    spreads = {'L0_attn_b_bq': (0.0, 0.564),
     'L0_attn_b_bk': (0.0, 2.0),
     'L0_attn_b_bv': (0.0, 0.1),
     'L0_attn_b_bo': (0.0, 0.1),
     'L0_ffn_b1': (0.0, 0.8),
     'L0_ffn_b2': (0.0, 0.293)}
    factors = {'L0_attn_a_Wq': 8.0,
     'L0_attn_a_bq': 8.0,
     'L0_attn_a_Wk': 8.0,
     'L0_attn_a_bk': 64.0,
     'L0_attn_a_Wv': 8.0,
     'L0_attn_a_bv': 8.0,
     'L0_attn_a_Wp': 8.0,
     'L0_attn_b_rel_emb': 24.204,
     'L0_ffn_w1': 3.206,
     'L0_ffn_w2': 2.883}
    for name, (base, spread) in spreads.items():
        noise = np.random.default_rng([zlib.crc32(name.encode()), seed]).standard_normal(out[name].shape)
        drawn = base * np.exp(spread * noise) if base else spread * noise
        out[name] = jnp.asarray(drawn.astype(out[name].dtype))
    for name, factor in factors.items():
        out[name] = (out[name] * factor).astype(out[name].dtype)
    return out
```

```python
from contextlib import ExitStack

import concourse.bass as bass
from concourse import mybir

F32 = mybir.dt.float32
F16 = mybir.dt.float16
I32 = mybir.dt.int32
ALU = mybir.AluOpType
ACT = mybir.ActivationFunctionType
AX = mybir.AxisListType

P = 128
B, T, D = 16, 256, 128
NT = B * T
TILES = NT // P
HEADS, DH = 16, 8
G = 4
SLOTS = HEADS // G
KH = T // P
NB = 2
GROUPS = B // NB
GT = NB * T
EXPERTS, HID = 8, 512
HC = HID // P
BLOCKS = NT // 512
GATED = 4 * 128 * 6
EPS = 1e-5
REL = 2 * T - 1
REL_MAX = 128
MROW = 24
MSCALE = 256.0
SCALE = float(DH) ** -0.5
ONE = 1
BLK = 13


class Setup:

    def __init__(self, sem):
        self.x = sem("x")
        self.consts = sem("consts")
        self.weights = sem("weights")
        self.alpha = sem("alpha")
        self.sign = sem("sign")
        self.binar = sem("binar")
        self.tr = sem("tr")
        self.evac = sem("evac")
        self.split = sem("split")
        self.bprow = sem("bprow")
        self.ready = sem("ready")
        self.ones = sem("ones")


class LayerNorm:

    def __init__(self, sem):
        self.stats = sem("stats")
        self.col = sem("col")
        self.sqrt = sem("sqrt")
        self.rstd = sem("rstd")
        self.normed = sem("normed")
        self.high = sem("high")
        self.logit = sem("logit")
        self.low = sem("low")
        self.logit_out = sem("logit_out")
        self.tr = sem("tr")
        self.begun = [self.low, self.logit_out, self.tr]


class Attention:

    def __init__(self, sem):
        self.proj = sem("proj")
        self.evac = sem("evac")
        self.t16 = sem("t16")
        self.v = sem("v")
        self.v_out = sem("v_out")
        self.e = sem("e")
        self.e_high = sem("e_high")
        self.e_low = sem("e_low")
        self.s1 = sem("s1")
        self.s1_used = sem("s1_used")
        self.r2 = sem("r2")
        self.rt = sem("rt")
        self.m3 = sem("m3")
        self.m3h = sem("m3h")
        self.m_row = sem("m_row")
        self.den = sem("den")
        self.rden = sem("rden")
        self.pp = sem("pp")
        self.o_copy = sem("o_copy")
        self.x_new = sem("x_new")
        self.exp = sem("exp")
        self.s2 = sem("s2")
        self.qm = sem("qm")
        self.pv = sem("pv")
        self.split = sem("split")
        self.a = sem("a")
        self.begun = [self.o_copy, self.x_new, self.exp, self.s2, self.qm, self.pv, self.split, self.a]


class Threshold:

    def __init__(self, sem):
        self.cnt = sem("cnt")
        self.tot = sem("tot")
        self.step = sem("step")
        self.gate = sem("gate")


class Experts:

    def __init__(self, sem):
        self.gst = sem("gst")
        self.gT = sem("gT")
        self.gTs = sem("gTs")
        self.b2 = sem("b2")
        self.mm1 = sem("mm1")
        self.high = sem("high")
        self.gelu = sem("gelu")
        self.gated = sem("gated")
        self.b2_used = sem("b2_used")
        self.mm2 = sem("mm2")
        self.low = sem("low")
        self.begun = [self.gelu, self.gated, self.b2_used, self.mm2, self.low]


def network(nc, x, wa, wb, bias_a, bias_b, bv_a, bv_b, bp_a, bp_b, rel, masks, ident, sel, gate, w1, b1, w2, b2, out):
    with ExitStack() as ctx:
        def sb(name, shape, dt):
            return ctx.enter_context(nc.sbuf_tensor(name, shape, dt))

        xs = sb("xs", [P, NT], F32)
        xh = sb("xh", [P, NT], F16)
        xl = sb("xl", [P, NT], F16)
        lnv = sb("lnv", [P, 8, TILES], F32)
        ident32 = sb("ident32", [P, P], F32)
        ident16 = sb("ident16", [P, P], F16)
        sel32 = sb("sel32", [P, P], F32)
        ones16 = sb("ones16", [P, P], F16)
        mask = sb("mask", [P, 2], F32)
        wth = [sb(f"wth{n}", [P, 9 * P], F16) for n in "ab"]
        wtl = [sb(f"wtl{n}", [P, 9 * P], F16) for n in "ab"]
        wpt = [sb(f"wpt{n}", [P, SLOTS * P], F32) for n in "ab"]
        qkb = [sb(f"qkb{n}", [P, 2 * SLOTS], F32) for n in "ab"]
        bv = [sb(f"bv{n}", [P, P], F32) for n in "ab"]
        zero32 = sb("zero32", [P, 1], F32)
        zero16 = sb("zero16", [P, 1], F16)
        alpha = sb("alpha", [P, BLK], F32)
        alphap = sb("alphap", [P, 1], F32)
        relh = sb("relh", [P, REL], F16)
        gth = sb("gth", [P, EXPERTS], F16)
        gtl = sb("gtl", [P, EXPERTS], F16)
        gt32 = sb("gt32", [P, EXPERTS], F32)
        b1s = sb("b1s", [P, EXPERTS * HC], F32)
        b2s = sb("b2s", [EXPERTS, D], F32)
        w1h, w1l, w2h, w2l = (sb(n, [P, EXPERTS * HID], F16) for n in ("w1h", "w1l", "w2h", "w2l"))
        qm = sb("qm", [P, NB * HEADS * T], F16)
        ks = sb("ks", [P, SLOTS * GT], F16)
        qs = sb("qs", [P, SLOTS * GT], F16)
        x32 = sb("x32", [P, 4, 512], F32)
        vp = sb("vp", [P, NB * KH * HEADS * 32], F32)
        pt = sb("pt", [P, 2, 2, 1024], F32)
        t16 = pt[:, 1, 1, 0:512].bitcast(F16).rearrange("p (a b) -> p a b", a=2)
        rmax = sb("rmax", [P, 2, KH, P], F32)
        r2 = sb("r2", [P, 2, P], F32)
        m3 = sb("m3", [P, 2, 32], F32)
        m3h = sb("m3h", [P, 2, 32], F16)
        osb = x32[:, 0:2, :].rearrange("p a b -> p (a b)")
        asb = x32[:, 2:4, :].rearrange("p a b -> p (a b)")
        lg = sb("lg", [P, TILES * EXPERTS], F32)
        cnt = sb("cnt", [P, 1], F16)
        tv = sb("tv", [P, 8], F32)
        ti = sb("ti", [P, 4], I32)
        big = sb("big", [P, 32768], F16)

        raw1 = big[:, 0:8192].bitcast(F32)
        raw2 = big[:, 8192:16384].bitcast(F32)
        rawa = big[:, 16384:16384 + 2 * BLK * P].bitcast(F32)
        rawb = big[:, 20480:20480 + 2 * BLK * P].bitcast(F32)
        rawr = big[:, 24576:24576 + 2 * REL].bitcast(F32)
        tmp = big[:, 26624:26624 + 2 * 512].bitcast(F32)
        tmp16 = big[:, 27648:27648 + 512]
        eh = big[:, 0:16384]
        el = big[:, 16384:32768]
        h32 = big[:, 0:4096].bitcast(F32)
        hh = big[:, 4096:8192]
        hl = big[:, 8192:12288]
        hh2 = big[:, 12288:16384]
        hl2 = big[:, 16384:20480]
        gst = big[:, 20480:20544].bitcast(F32)
        gtt = big[0:EXPERTS, 20544:21568].bitcast(F32)
        xn = big[:, 28672:30720].bitcast(F32).rearrange("p (a b) -> p a b", a=2)
        stats = big[:, 30720:30720 + 12 * TILES].bitcast(F32).rearrange("p (t s) -> p t s", s=6)
        zt = big[:, 31232:31744].bitcast(F32)
        junk = big[:, 31744:32000]

        ps = ctx.enter_context(nc.psum_tensor("ps", [P, 8, 512], F32))

        def region(r):
            return ps[:, 2 * r:2 * r + 2, :].rearrange("p a b -> p (a b)")

        O = ps[:, 4:6, :].rearrange("p a b -> p (a b)")

        def sem(phase):
            return lambda name: ctx.enter_context(nc.semaphore(f"{phase}_{name}"))

        su = Setup(sem("setup"))
        LN = [LayerNorm(sem(f"ln{n}")) for n in range(4)]
        AT = [Attention(sem(f"attn{n}")) for n in "ab"]
        TH = [Threshold(sem(f"thr{n}")) for n in range(2)]
        FF = [Experts(sem(f"ffn{n}")) for n in range(2)]
        out_done = ctx.enter_context(nc.semaphore("out_done"))

        block = ctx.enter_context(nc.Block())

        def pair(t, n, slot, half):
            o = n * HEADS * T
            return t[:, o:o + HEADS * T].rearrange("p (g s q) -> p g s q", g=G, s=SLOTS)[
                :, 2 * half:2 * half + 2, slot, :]

        @block.sync
        def _(sp):
            for n in range(4):
                sp.dma_start(xs[:, 1024 * n:1024 * n + 1024], x[:, 1024 * n:1024 * n + 1024]).then_inc(su.x, 16)
            for dst, src in ((ident32, ident), (sel32, sel), (mask, masks), (qkb[0], bias_a), (qkb[1], bias_b),
                             (bv[0], bv_a), (bv[1], bv_b), (gt32, gate), (b1s, b1), (b2s, b2)):
                sp.dma_start(dst[:], src).then_inc(su.consts, 16)
            for dst, src in ((rawa, wa), (rawb, wb), (rawr, rel), (raw1, w1), (raw2, w2)):
                sp.dma_start(dst, src).then_inc(su.weights, 16)
            for s in (*LN, *AT, *FF):
                for sem in s.begun:
                    sp.sem_inc(sem, ONE)
            sp.wait_ge(su.evac, 2 * BLK)
            sp.dma_start(wpt[0][8:9, 0:P], bp_a).then_inc(su.bprow, 16)
            sp.dma_start(wpt[1][8:9, 0:P], bp_b).then_inc(su.bprow, 16)

            for a in range(2):
                s = AT[a]
                with sp.Fori(0, GROUPS) as i:
                    for b in range(NB):
                        sp.wait_ge(s.m3h, NB * i + b + 1)
                        for g in range(G):
                            o = b * HEADS * T
                            dst = qm[32 * g + MROW:32 * g + MROW + 1, o + g * SLOTS * T:o + (g + 1) * SLOTS * T]
                            sp.dma_start(dst.rearrange("p (k q) -> p k q", q=32), m3h[32 * g:32 * g + 32, b, :])\
                              .then_inc(s.m_row, 16)
            sp.wait_ge(FF[1].gated, ONE + BLOCKS * EXPERTS)
            for n in range(4):
                sp.dma_start(out[:, 1024 * n:1024 * n + 1024], xs[:, 1024 * n:1024 * n + 1024]).then_inc(out_done, 16)
            sp.wait_ge(out_done, 64)

        def pe_setup(pe):
            pe.wait_ge(su.consts, 160)
            pe.wait_ge(su.weights, 80)
            for k in range(2 * BLK):
                raw = rawa if k < BLK else rawb
                if k == 0:
                    pe.wait_ge(su.binar, 2)
                if k >= 2:
                    pe.wait_ge(su.evac, k - 1)
                kk = k % BLK
                nc.tensor.transpose(ps[:, k % 2, 0:P], raw[:, kk * P:kk * P + P], ident32[:]).then_inc(su.tr, 1)

        def pe_ln(pe, s, logits, first):
            with pe.Fori(0, 4) as i:
                for j in range(2):
                    pe.wait_ge(s.normed, 2 * i + j + 1)
                    if j == 0:
                        pe.wait_ge(s.low, ONE + 2 * i)
                    else:
                        pe.wait_ge(s.low, ONE + 2 * i)
                    for t in range(4):
                        m = nc.tensor.transpose(ps[:, j, t * P:t * P + P], xn[:, j, t * P:t * P + P], ident32[:])
                    m.then_inc(s.tr, 1)
                    if logits:
                        pe.wait_ge(s.low, ONE + 2 * i + j + 1)
                        pe.wait_ge(s.logit_out, ONE + 2 * i)
                        for t in range(4):
                            c = (i * 8 + j * 4 + t) * P
                            o = ps[:, 2 + j, t * EXPERTS:(t + 1) * EXPERTS]
                            nc.tensor.matmul(o, xh[:, bass.ds(c, P)], gth[:], start=True, stop=False)
                            nc.tensor.matmul(o, xh[:, bass.ds(c, P)], gtl[:], start=False, stop=False)
                            m = nc.tensor.matmul(o, xl[:, bass.ds(c, P)], gth[:], start=False, stop=True)
                        m.then_inc(s.logit, 1)

        def pe_attn(pe, a):
            s = AT[a]
            rel_on = a == 1
            units = 2 * SLOTS

            def scores(i, b, slot, half, r, second):
                for kh in range(KH):
                    o = region(r)[:, 512 * kh:512 * kh + 512].rearrange("p (g q) -> p g q", g=2)
                    kcol = slot * GT + b * T + kh * P
                    m = nc.tensor.matmul(o, ks[:, kcol:kcol + P], pair(qm, b, slot, half), start=True,
                                         stop=not rel_on)
                    if rel_on:
                        m = nc.tensor.matmul(o, ident16[:], pair(eh, kh * NB + b, slot, half), start=False, stop=not second)
                        if second:
                            m = nc.tensor.matmul(o, ident16[:], pair(el, kh * NB + b, slot, half), start=False, stop=True)
                return m

            def max_transpose(i, b):
                pe.wait_ge(s.r2, NB * i + b + 1)
                nc.tensor.transpose(ps[:, 6 + b, 0:P], r2[:, b, :], ident32[:]).then_inc(s.rt, 1)

            def pv(i, b, slot):
                pe.wait_ge(s.exp, ONE + units * (NB * i + b) + 2 * slot + 2)
                if slot == 0:
                    pe.wait_ge(s.o_copy, ONE + NB * i + b)
                    pe.wait_ge(s.v_out, NB * KH * (i + 1))
                for kh in range(KH):
                    for g in range(G):
                        v0 = ((b * KH + kh) * HEADS + slot * G + g) * 32
                        p0 = kh * 512 + (g % 2) * T
                        m = nc.tensor.matmul(O[32 * g:32 * g + 32, slot * T:slot * T + T], vp[:, v0:v0 + 32],
                                             pt[:, slot % 2, g // 2, p0:p0 + T], start=kh == 0, stop=kh == KH - 1,
                                             tile_position=(0, 32 * g))
                m.then_inc(s.pv, 1)

            def second_pass(i, b):
                n = NB * i + b
                pe.wait_ge(s.m_row, 64 * (n + 1))
                for slot in range(SLOTS):
                    for half in range(2):
                        u = 2 * slot + half
                        if u < 2:
                            pe.wait_ge(s.s1_used, units * NB * (i + 1))
                            if b:
                                pe.wait_ge(s.exp, ONE + units * n + u - 1)
                        else:
                            pe.wait_ge(s.exp, ONE + units * n + u - 1)
                        scores(i, b, slot, half, half, True).then_inc(s.s2, 1)
                    if slot:
                        pv(i, b, slot - 1)
                    if b == 0 and slot == 0:
                        max_transpose(i, 1)
                pv(i, b, SLOTS - 1)

            def project(i, b):
                n = NB * i + b
                pe.wait_ge(s.o_copy, ONE + n + 1)
                pe.wait_ge(s.m3, NB * (i + 1))
                pe.wait_ge(s.x_new, ONE + n)
                for j in range(2):
                    m = nc.tensor.matmul(ps[:, 6 + j, :], sel32[:], osb[:, 512 * j:512 * j + 512], start=True, stop=True)
                m.then_inc(s.den, 1)
                pe.wait_ge(s.a, ONE + n + 1)
                for t in range(2):
                    for slot in range(SLOTS):
                        m = nc.tensor.matmul(ps[:, 6, t * P:t * P + P], asb[:, slot * T + t * P:slot * T + t * P + P],
                                             wpt[a][:, slot * P:slot * P + P], start=slot == 0, stop=slot == SLOTS - 1)
                m.then_inc(s.pp, 1)

            pe.wait_ge(LN[2 * a].low, ONE + 8)
            with pe.Fori(0, GROUPS) as i:
                for c in range(2 * SLOTS):
                    if c == 0:
                        pe.wait_ge(s.x_new, ONE + NB * i)
                    elif c >= 2:
                        pe.wait_ge(s.evac, 2 * SLOTS * i + c - 1)
                    tok = bass.ds(i * GT, GT)
                    o = ps[:, 6 + c % 2, :]
                    w = slice(c * P, c * P + P)
                    nc.tensor.matmul(o, wth[a][:, w], xh[:, tok], start=True, stop=False)
                    nc.tensor.matmul(o, wth[a][:, w], xl[:, tok], start=False, stop=False)
                    nc.tensor.matmul(o, wtl[a][:, w], xh[:, tok], start=False, stop=True).then_inc(s.proj, 1)
                pe.wait_ge(s.evac, 2 * SLOTS * i + 2 * SLOTS - 1)
                w = slice(8 * P, 9 * P)
                for t in range(NB * KH):
                    tok = bass.ds(i * GT + t * P, P)
                    o = ps[:, 6, t * P:t * P + P]
                    nc.tensor.matmul(o, xh[:, tok], wth[a][:, w], start=True, stop=False)
                    nc.tensor.matmul(o, xh[:, tok], wtl[a][:, w], start=False, stop=False)
                    m = nc.tensor.matmul(o, xl[:, tok], wth[a][:, w], start=False, stop=True)
                m.then_inc(s.v, 1)
                pe.wait_ge(s.qm, ONE + NB * G * (i + 1))
                if rel_on:
                    for u in range(KH * 8):
                        kh, qc = u // 8, u % 8
                        if u < 2:
                            pe.wait_ge(s.exp, ONE + units * NB * i)
                        else:
                            pe.wait_ge(s.e_low, KH * 8 * i + u - 1)
                        for q in range(32):
                            w0 = T - 1 - (qc * 32 + q) + kh * P
                            m = nc.tensor.matmul(region(u % 2)[:, q * 32:q * 32 + 32], relh[:, w0:w0 + P],
                                                 qm[:, qc * 32 + q:qc * 32 + q + (NB * HEADS - 1) * T + 1:T],
                                                 start=True, stop=True)
                        m.then_inc(s.e, 1)
                for b in range(NB):
                    for slot in range(SLOTS):
                        for half in range(2):
                            u = units * b + 2 * slot + half
                            if u < 2:
                                if rel_on:
                                    pe.wait_ge(s.e_low, KH * 8 * (i + 1))
                                else:
                                    pe.wait_ge(s.exp, ONE + units * NB * i)
                            else:
                                pe.wait_ge(s.s1_used, units * NB * i + u - 1)
                            if u == 0:
                                pe.wait_ge(s.split, ONE + 2 * SLOTS * (i + 1))
                            scores(i, b, slot, half, u % 2, False).then_inc(s.s1, 1)
                        if b == 1 and slot == 1:
                            pe.wait_ge(s.v_out, NB * KH * (i + 1))
                            max_transpose(i, 0)
                second_pass(i, 0)
                second_pass(i, 1)
                project(i, 0)
                project(i, 1)

        def pe_threshold(pe, s):
            with pe.Fori(0, 32) as i:
                pe.wait_ge(s.cnt, i + 1)
                nc.tensor.matmul(ps[:, 6, 0:1], ones16[:], cnt[:], start=True, stop=True).then_inc(s.tot, 1)

        def pe_ffn(pe, s, ln):
            def up(i, e):
                for c in range(HC):
                    n = EXPERTS * HC * i + HC * e + c
                    if e:
                        pe.wait_ge(s.gelu, ONE + n - HC + 1)
                    else:
                        pe.wait_ge(s.gelu, ONE + EXPERTS * HC * i)
                    w = slice(e * HID + c * P, e * HID + c * P + P)
                    tok = bass.ds(i * 512, 512)
                    nc.tensor.matmul(ps[:, c, :], w1h[:, w], xh[:, tok], start=True, stop=False)
                    nc.tensor.matmul(ps[:, c, :], w1h[:, w], xl[:, tok], start=False, stop=False)
                    nc.tensor.matmul(ps[:, c, :], w1l[:, w], xh[:, tok], start=False, stop=True).then_inc(s.mm1, 1)

            def down(i, e):
                hi, lo = ((hh, hl), (hh2, hl2))[e % 2]
                pe.wait_ge(s.low, ONE + HC * (EXPERTS * i + e + 1))
                pe.wait_ge(s.high, HC * (EXPERTS * i + e + 1))
                if e >= 2:
                    pe.wait_ge(s.gated, ONE + EXPERTS * i + e - 1)
                else:
                    pe.wait_ge(s.gated, ONE + EXPERTS * i)
                for t in range(4):
                    for c in range(HC):
                        h = slice(c * 512 + t * P, c * 512 + t * P + P)
                        w = slice((e * HC + c) * P, (e * HC + c + 1) * P)
                        o = ps[:, 4 + e % 2, t * P:t * P + P]
                        nc.tensor.matmul(o, hi[:, h], w2h[:, w], start=c == 0, stop=False)
                        nc.tensor.matmul(o, hi[:, h], w2l[:, w], start=False, stop=False)
                        m = nc.tensor.matmul(o, lo[:, h], w2h[:, w], start=False, stop=c == HC - 1)
                m.then_inc(s.mm2, 1)

            pe.wait_ge(ln.low, ONE + 8)
            pe.wait_ge(ln.logit_out, ONE + 8)
            with pe.Fori(0, BLOCKS) as i:
                up(i, 0)
                pe.wait_ge(s.gst, i + 1)
                pe.wait_ge(s.b2_used, ONE + i)
                for t in range(4):
                    m = nc.tensor.transpose(ps[0:EXPERTS, 6, t * P:t * P + P], gst[:, t * EXPERTS:(t + 1) * EXPERTS],
                                            ident32[:])
                m.then_inc(s.gT, 1)
                for e in range(1, EXPERTS):
                    up(i, e)
                    if e == 1:
                        pe.wait_ge(s.gTs, i + 1)
                        for t in range(4):
                            m = nc.tensor.matmul(ps[:, 7, t * P:t * P + P], gtt[:, t * P:t * P + P], b2s[:],
                                                 start=True, stop=True)
                        m.then_inc(s.b2, 1)
                    down(i, e - 1)
                down(i, EXPERTS - 1)

        @block.tensor
        def _(pe):
            pe_setup(pe)
            pe.wait_ge(su.evac, 2 * BLK)
            pe.wait_ge(su.bprow, 32)
            pe.wait_ge(su.split, 1)
            pe_ln(pe, LN[0], False, True)
            pe_attn(pe, 0)
            pe_ln(pe, LN[1], True, False)
            pe_threshold(pe, TH[0])
            pe_ffn(pe, FF[0], LN[1])
            pe_ln(pe, LN[2], False, False)
            pe_attn(pe, 1)
            pe_ln(pe, LN[3], True, False)
            pe_threshold(pe, TH[1])
            pe_ffn(pe, FF[1], LN[3])

        def act_ln(act, s):
            act.wait_ge(s.col, 1)
            nc.scalar.activation(lnv[:, 3, :], lnv[:, 2, :], ACT.Sqrt).then_inc(s.sqrt, 1)
            with act.Fori(0, 4) as i:
                for j in range(2):
                    act.wait_ge(s.tr, ONE + 2 * i + j + 1)
                    nc.scalar.activation(xh[:, bass.ds(i * 1024 + j * 512, 512)], ps[:, j, :], ACT.Copy)\
                      .then_inc(s.high, 1)

        def act_attn(act, a):
            s = AT[a]
            with act.Fori(0, GROUPS) as i:
                for c in range(2 * SLOTS):
                    act.wait_ge(s.proj, 2 * SLOTS * i + c + 1)
                    if c >= 4:
                        act.wait_ge(s.split, ONE + 2 * SLOTS * i + c - 3)
                    else:
                        act.wait_ge(s.split, ONE + 2 * SLOTS * i)
                    nc.scalar.activation(x32[:, c % 4, :], ps[:, 6 + c % 2, :], ACT.Identity,
                                         bias=qkb[a][:, c:c + 1]).then_inc(s.evac, 1)
                if a == 1:
                    act.wait_ge(s.pv, ONE + NB * SLOTS * i)
                    for u in range(KH * 8):
                        kh, qc = u // 8, u % 8
                        act.wait_ge(s.e, KH * 8 * i + u + 1)
                        src = region(u % 2).rearrange("p (q n) -> p n q", q=32)
                        dst = eh[:, kh * 8192:kh * 8192 + 8192].rearrange("p (n q) -> p n q", q=T)[
                            :, :, qc * 32:qc * 32 + 32]
                        nc.scalar.activation(dst, src, ACT.Copy).then_inc(s.e_high, 1)
                for b in range(NB):
                    for slot in range(SLOTS):
                        for half in range(2):
                            n = NB * i + b
                            act.wait_ge(s.s2, ONE + 8 * n + 2 * slot + half + 1)
                            if half == 0 and n is not None:
                                if slot >= 2:
                                    act.wait_ge(s.pv, ONE + SLOTS * n + slot - 1)
                                else:
                                    act.wait_ge(s.pv, ONE + SLOTS * n)
                            nc.scalar.activation(pt[:, slot % 2, half, :], region(half), ACT.Exp, scale=SCALE)\
                              .then_inc(s.exp, 1)
                    act.wait_ge(s.pv, ONE + SLOTS * (NB * i + b + 1))
                    act.wait_ge(s.a, ONE + NB * i + b)
                    nc.scalar.activation(osb, O, ACT.Copy).then_inc(s.o_copy, 1)

        def act_ffn(act, s):
            with act.Fori(0, BLOCKS) as i:
                for e in range(EXPERTS):
                    for c in range(HC):
                        n = EXPERTS * HC * i + HC * e + c
                        act.wait_ge(s.mm1, n + 1)
                        if e:
                            act.wait_ge(s.low, ONE + n - HC + 1)
                        else:
                            act.wait_ge(s.low, ONE + EXPERTS * HC * i)
                        nc.scalar.activation(h32[:, c * 512:c * 512 + 512], ps[:, c, :], ACT.Gelu_apprx_tanh,
                                             bias=b1s[:, e * HC + c:e * HC + c + 1]).then_inc(s.gelu, 1)

        @block.scalar
        def _(act):
            act.wait_ge(su.weights, 80)
            act.wait_ge(su.ones, 3)
            nc.scalar.activation(pt[:, 0, :, :].rearrange("p a b -> p (a b)")[:, 0:BLK * P], rawa, ACT.Sign)\
              .then_inc(su.sign, 1)
            for n in range(4):
                act_ln(act, LN[n])
                if n % 2 == 0:
                    act_attn(act, n // 2)
                else:
                    act_ffn(act, FF[n // 2])

        def dve_setup(v):
            sg = pt[:, 0, :, :].rearrange("p a b -> p (a b)")[:, 0:BLK * P]
            nc.vector.memset(vp[:], 0.0).then_inc(su.ones, 1)
            nc.vector.memset(ones16[:], 1.0).then_inc(su.ones, 1)
            v.wait_ge(su.ones, 2)
            nc.vector.memset(vp[:].rearrange("p (n c) -> p n c", c=32)[:, :, 8:9], 1.0).then_inc(su.ones, 1)
            v.wait_ge(su.weights, 80)
            v.wait_ge(su.consts, 160)
            nc.vector.tensor_copy(ident16[:], ident32[:]).then_inc(su.alpha, 1)
            nc.vector.tensor_reduce(alpha[:], rawa.rearrange("p (n c) -> p n c", c=P), AX.X, ALU.add,
                                    apply_absolute_value=True).then_inc(su.alpha, 1)
            v.wait_ge(su.alpha, 2)
            nc.vector.tensor_reduce(alphap[:], alpha[:, 9:13], AX.X, ALU.add).then_inc(su.alpha, 1)
            v.wait_ge(su.alpha, 3)
            nc.vector.tensor_scalar(alpha[:, 0:9], alpha[:, 0:9], 1.0 / D, None, ALU.mult).then_inc(su.alpha, 1)
            nc.vector.tensor_scalar(alphap[:], alphap[:], 1.0 / D, None, ALU.mult).then_inc(su.alpha, 1)
            v.wait_ge(su.sign, 1)
            v.wait_ge(su.alpha, 5)
            nc.vector.tensor_tensor(sg, sg, rawa, ALU.subtract).then_inc(su.alpha, 1)
            v.wait_ge(su.alpha, 6)
            nc.vector.tensor_tensor(rawa, rawa, sg, ALU.add).then_inc(su.alpha, 1)
            v.wait_ge(su.alpha, 7)
            qkv = rawa[:, 0:9 * P].rearrange("p (n c) -> p n c", c=P)
            nc.vector.tensor_tensor(qkv, qkv, alpha[:, 0:9].unsqueeze(2).broadcast_to([P, 9, P]), ALU.mult)\
              .then_inc(su.binar, 1)
            nc.vector.tensor_scalar(rawa[:, 9 * P:13 * P], rawa[:, 9 * P:13 * P], alphap[:, 0:1], None, ALU.mult)\
              .then_inc(su.binar, 1)
            for k in range(2 * BLK):
                a, kk = k // BLK, k % BLK
                v.wait_ge(su.tr, k + 1)
                src = ps[:, k % 2, 0:P]
                if kk < 9:
                    w = slice(kk * P, kk * P + P)
                    nc.vector.tensor_copy(wth[a][:, w], src).then_inc(su.alpha, 1)
                    v.wait_ge(su.alpha, 8 + 9 * a + kk)
                    nc.vector.tensor_tensor(wtl[a][:, w], src, wth[a][:, w], ALU.subtract).then_inc(su.evac, 1)
                else:
                    w = slice((kk - 9) * P, (kk - 8) * P)
                    nc.vector.tensor_copy(wpt[a][:, w], src).then_inc(su.evac, 1)
            n = 7 + 18
            for hi, lo, raw in ((w1h, w1l, raw1), (w2h, w2l, raw2), (gth, gtl, gt32[:])):
                nc.vector.tensor_copy(hi[:], raw).then_inc(su.alpha, 1)
                n += 1
                v.wait_ge(su.alpha, n)
                nc.vector.tensor_tensor(lo[:], raw, hi[:], ALU.subtract).then_inc(su.alpha, 1)
                n += 1
            nc.vector.tensor_copy(tmp16[:, 0:REL], rawr).then_inc(su.alpha, 1)
            n += 1
            v.wait_ge(su.alpha, n)
            nc.vector.scalar_tensor_tensor(out=relh[:], in0=tmp16[:, 0:REL], scalar=mask[:, 1:2], in1=rawr,
                                           op0=ALU.mult, op1=ALU.add).then_inc(su.split, 1)

        def dve_ln(v, s, logits):
            with v.Fori(0, 4) as i:
                for j in range(8):
                    m = nc.vector.bn_stats(stats[:, bass.ds(i * 8 + j, 1), :].rearrange("p a b -> p (a b)"),
                                           xs[:, bass.ds((i * 8 + j) * P, P)])
                    m.then_inc(s.stats, 1)
            v.wait_ge(s.stats, TILES)
            n = [0]

            def link(m):
                n[0] += 1
                m.then_inc(s.rstd, 1)
                v.wait_ge(s.rstd, n[0])

            me, ve, mo, vo = (stats[:, :, k] for k in (1, 2, 4, 5))
            c = [lnv[:, k, :] for k in range(8)]
            link(nc.vector.tensor_tensor(c[0], me, mo, ALU.add))
            link(nc.vector.tensor_tensor(c[1], me, mo, ALU.subtract))
            link(nc.vector.tensor_tensor(c[4], ve, vo, ALU.add))
            link(nc.vector.tensor_scalar(c[0], c[0], 0.5, None, ALU.mult))
            link(nc.vector.tensor_tensor(c[1], c[1], c[1], ALU.mult))
            link(nc.vector.tensor_scalar(c[4], c[4], 1.0 / D, EPS, ALU.mult, ALU.add))
            nc.vector.scalar_tensor_tensor(out=c[2], in0=c[1], scalar=0.25, in1=c[4], op0=ALU.mult, op1=ALU.add)\
              .then_inc(s.col, 1)
            v.wait_ge(s.sqrt, 1)
            link(nc.vector.reciprocal(c[5], c[3]))
            v.wait_ge(s.col, 1)
            link(nc.vector.tensor_tensor(c[6], c[5], c[5], ALU.mult))
            link(nc.vector.tensor_tensor(c[6], c[6], c[2], ALU.mult))
            link(nc.vector.tensor_scalar(c[6], c[6], -0.5, 1.5, ALU.mult, ALU.add))
            link(nc.vector.tensor_tensor(c[7], c[6], c[5], ALU.mult))
            with v.Fori(0, 4) as i:
                for j in range(2):
                    v.wait_ge(s.tr, ONE + 2 * i)
                    for t in range(4):
                        k = i * 8 + j * 4 + t
                        m = nc.vector.tensor_scalar(xn[:, j, t * P:t * P + P], xs[:, bass.ds(k * P, P)],
                                                    lnv[:, 0, bass.ds(k, 1)], lnv[:, 7, bass.ds(k, 1)],
                                                    ALU.subtract, ALU.mult)
                    m.then_inc(s.normed, 1)
                for j in range(2):
                    v.wait_ge(s.high, 2 * i + j + 1)
                    c0 = i * 1024 + j * 512
                    nc.vector.tensor_tensor(xl[:, bass.ds(c0, 512)], ps[:, j, :], xh[:, bass.ds(c0, 512)],
                                            ALU.subtract).then_inc(s.low, 1)
                if logits:
                    for j in range(2):
                        v.wait_ge(s.logit, 2 * i + j + 1)
                        nc.vector.tensor_copy(lg[:, bass.ds((i * 2 + j) * 32, 32)], ps[:, 2 + j, 0:32])\
                          .then_inc(s.logit_out, 1)

        def dve_attn(v, a):
            s = AT[a]
            step = 2 * SLOTS

            def maxima(i, b):
                v.wait_ge(s.rt, NB * i + b + 1)
                nc.vector.tensor_reduce(m3[:, b, :], ps[:, 6 + b, 0:P].rearrange("p (k q) -> p q k", k=4), AX.X,
                                        ALU.max).then_inc(s.m3, 1)
                v.wait_ge(s.m3, NB * i + b + 1)
                nc.vector.tensor_scalar(m3h[:, b, :], m3[:, b, :], -1.0 / MSCALE, None, ALU.mult).then_inc(s.m3h, 1)

            with v.Fori(0, GROUPS) as i:
                v.wait_ge(s.s2, ONE + 16 * i)
                v.wait_ge(s.qm, ONE + NB * G * i)
                for c in range(step):
                    v.wait_ge(s.evac, step * i + c + 1)
                    nc.vector.tensor_copy(t16[:, c % 2, :], x32[:, c % 4, :]).then_inc(s.t16, 1)
                    dst, k = (qs, 0) if c < SLOTS else (ks, 1)
                    v.wait_ge(s.t16, step * i + c + 1)
                    nc.vector.scalar_tensor_tensor(out=dst[:, (c % SLOTS) * GT:(c % SLOTS + 1) * GT],
                                                   in0=t16[:, c % 2, :], scalar=mask[:, k:k + 1], in1=x32[:, c % 4, :],
                                                   op0=ALU.mult, op1=ALU.add).then_inc(s.split, 1)
                v.wait_ge(s.v, i + 1)
                v.wait_ge(s.pv, ONE + 8 * i)
                for t in range(NB * KH):
                    nc.vector.tensor_tensor(vp[:, t * 512:t * 512 + 512].rearrange("p (n c) -> p n c", c=32)[:, :, 0:DH],
                                            ps[:, 6, t * P:t * P + P].rearrange("p (n c) -> p n c", c=DH),
                                            bv[a][:].rearrange("p (n c) -> p n c", c=DH), ALU.add)\
                      .then_inc(s.v_out, 1)
                if a == 1:
                    for u in range(KH * 8):
                        kh, qc = u // 8, u % 8
                        v.wait_ge(s.e_high, KH * 8 * i + u + 1)
                        src = region(u % 2).rearrange("p (q n) -> p n q", q=32)
                        hi, lo = (t[:, kh * 8192:kh * 8192 + 8192].rearrange("p (n q) -> p n q", q=T)[
                            :, :, qc * 32:qc * 32 + 32] for t in (eh, el))
                        nc.vector.tensor_tensor(lo, src, hi, ALU.subtract).then_inc(s.e_low, 1)
                for b in range(NB):
                    for slot in range(SLOTS):
                        for half in range(2):
                            u = step * b + 2 * slot + half
                            v.wait_ge(s.s1, 16 * i + u + 1)
                            for kh in range(KH):
                                src = region(u % 2)[:, 512 * kh:512 * kh + 512].rearrange(
                                    "p (g q k) -> p g q k", g=2, k=32)
                                dst = rmax[:, b, kh, 64 * half:64 * half + 64].rearrange(
                                    "p (g q) -> p g q", g=2)[:, :, slot * 8:slot * 8 + 8]
                                m = nc.vector.tensor_reduce(dst, src, AX.X, ALU.max, apply_transpose=True)
                            m.then_inc(s.s1_used, 1)
                        if b == 1 and slot == 1:
                            maxima(i, 0)
                    v.wait_ge(s.s1_used, 16 * i + 8 * b + 8)
                    nc.vector.tensor_tensor(r2[:, b, :], rmax[:, b, 0, :], rmax[:, b, 1, :], ALU.max)\
                      .then_inc(s.r2, 1)
                maxima(i, 1)
                for b in range(NB):
                    n = NB * i + b
                    v.wait_ge(s.den, n + 1)
                    nc.vector.reciprocal(asb, ps[:, 6:8, :].rearrange("p a b -> p (a b)")).then_inc(s.rden, 1)
                    v.wait_ge(s.pp, n + 1)
                    xc = xs[:, bass.ds(i * GT + b * T, T)]
                    nc.vector.tensor_tensor(xc, xc, ps[:, 6, 0:T], ALU.add).then_inc(s.x_new, 1)

        def dve_threshold(v, s):
            n = [0]

            def link(m):
                n[0] += 1
                m.then_inc(s.step, 1)
                v.wait_ge(s.step, n[0])

            neg, sgn, need, bitf, unit = (tv[:, k:k + 1] for k in range(5))
            kth = tv[:, 5:6]
            have, got, nxt, cand = (ti[:, k:k + 1] for k in range(4))
            total = NT * EXPERTS
            nc.vector.tensor_scalar(junk, lg[:], 0.0, 0.0, ALU.is_lt, ALU.add, accum_out=cnt[:]).then_inc(s.cnt, 1)
            v.wait_ge(s.tot, 1)
            link(nc.vector.tensor_scalar(neg, ps[:, 6, 0:1], float(GATED), None, ALU.is_ge))
            link(nc.vector.tensor_scalar(sgn, neg, -2.0, 1.0, ALU.mult, ALU.add))
            link(nc.vector.tensor_scalar(need, neg, float(2 * GATED - total - 1), float(total - GATED + 1),
                                         ALU.mult, ALU.add))
            link(nc.vector.tensor_scalar(zt, lg[:], sgn, None, ALU.mult))
            link(nc.vector.memset(have, 0))
            link(nc.vector.memset(bitf, float(2 ** 30)))
            link(nc.vector.tensor_copy(cand, bitf))
            base = n[0]
            with v.Fori(0, 31) as i:
                v.wait_ge(s.step, base + 5 * i)
                nc.vector.tensor_scalar(junk, zt, cand.bitcast(F32), 0.0, ALU.is_ge, ALU.add,
                                        accum_out=cnt[:]).then_inc(s.cnt, 1)
                v.wait_ge(s.cnt, i + 2)
                nc.vector.tensor_scalar(nxt, bitf, 0.5, None, ALU.mult).then_inc(s.step, 1)
                v.wait_ge(s.tot, i + 2)
                nc.vector.tensor_scalar(got, ps[:, 6, 0:1], need, bitf, ALU.is_ge, ALU.mult).then_inc(s.step, 1)
                v.wait_ge(s.step, base + 5 * i + 2)
                nc.vector.tensor_scalar(bitf, bitf, 0.5, None, ALU.mult).then_inc(s.step, 1)
                nc.vector.tensor_tensor(have, have, got, ALU.bitwise_or).then_inc(s.step, 1)
                v.wait_ge(s.step, base + 5 * i + 4)
                nc.vector.tensor_tensor(cand, have, nxt, ALU.bitwise_or).then_inc(s.step, 1)
            n[0] = base + 5 * 31
            v.wait_ge(s.step, n[0])
            link(nc.vector.tensor_scalar(kth, have.bitcast(F32), sgn, None, ALU.mult))
            nc.vector.scalar_tensor_tensor(out=lg[:], in0=lg[:], scalar=kth, in1=lg[:], op0=ALU.is_ge, op1=ALU.mult)\
              .then_inc(s.gate, 1)
            v.wait_ge(s.gate, 1)

        def dve_ffn(v, s):
            def split(i, e):
                hi, lo = ((hh, hl), (hh2, hl2))[e % 2]
                if e < 2:
                    v.wait_ge(s.mm2, ONE + EXPERTS * i)
                else:
                    v.wait_ge(s.mm2, ONE + EXPERTS * i + e - 1)
                for c in range(HC):
                    n = EXPERTS * HC * i + HC * e + c
                    v.wait_ge(s.high, n + 1)
                    w = slice(c * 512, c * 512 + 512)
                    nc.vector.tensor_tensor(lo[:, w], h32[:, w], hi[:, w], ALU.subtract).then_inc(s.low, 1)

            def gated(i, e):
                v.wait_ge(s.mm2, ONE + EXPERTS * i + e + 1)
                if e:
                    v.wait_ge(s.gated, ONE + EXPERTS * i + e)
                else:
                    v.wait_ge(s.b2_used, ONE + i + 1)
                for t in range(4):
                    xc = xs[:, bass.ds(i * 512 + t * P, P)]
                    m = nc.vector.scalar_tensor_tensor(out=xc, in0=ps[:, 4 + e % 2, t * P:t * P + P],
                                                       scalar=gst[:, t * EXPERTS + e:t * EXPERTS + e + 1], in1=xc,
                                                       op0=ALU.mult, op1=ALU.add)
                m.then_inc(s.gated, 1)

            with v.Fori(0, BLOCKS) as i:
                v.wait_ge(s.gated, ONE + EXPERTS * i)
                nc.vector.tensor_copy(gst, lg[:, bass.ds(i * 32, 32)]).then_inc(s.gst, 1)
                v.wait_ge(s.gst, i + 1)
                split(i, 0)
                v.wait_ge(s.gT, i + 1)
                nc.vector.tensor_copy(gtt, ps[0:EXPERTS, 6, :]).then_inc(s.gTs, 1)
                v.wait_ge(s.b2, i + 1)
                xc = xs[:, bass.ds(i * 512, 512)]
                nc.vector.tensor_tensor(xc, xc, ps[:, 7, :], ALU.add).then_inc(s.b2_used, 1)
                for e in range(1, EXPERTS):
                    split(i, e)
                    gated(i, e - 1)
                gated(i, EXPERTS - 1)

        @block.vector
        def _(v):
            dve_setup(v)
            v.wait_ge(su.x, 64)
            dve_ln(v, LN[0], False)
            dve_attn(v, 0)
            v.wait_ge(AT[0].x_new, ONE + B)
            dve_ln(v, LN[1], True)
            v.wait_ge(LN[1].logit_out, ONE + 8)
            dve_threshold(v, TH[0])
            dve_ffn(v, FF[0])
            v.wait_ge(FF[0].gated, ONE + BLOCKS * EXPERTS)
            dve_ln(v, LN[2], False)
            dve_attn(v, 1)
            v.wait_ge(AT[1].x_new, ONE + B)
            dve_ln(v, LN[3], True)
            v.wait_ge(LN[3].logit_out, ONE + 8)
            dve_threshold(v, TH[1])
            dve_ffn(v, FF[1])

        @block.gpsimd
        def _(pool):
            nc.gpsimd.memset(qm[:], 0.0).then_inc(su.ready, 1)
            nc.gpsimd.memset(zero32[:], 0.0).then_inc(su.ready, 1)
            nc.gpsimd.memset(zero16[:], 0.0).then_inc(su.ready, 1)
            pool.wait_ge(su.ready, 3)
            for a in range(2):
                s = AT[a]
                with pool.Fori(0, GROUPS) as i:
                    pool.wait_ge(s.s2, ONE + 16 * i)
                    pool.wait_ge(s.split, ONE + 2 * SLOTS * i + SLOTS)
                    for b in range(NB):
                        for g in range(G):
                            rows = slice(32 * g, 32 * g + 32)
                            src = qs[rows, :].rearrange("p (s t) -> p s t", s=SLOTS)[:, :, b * T:b * T + T]
                            o = b * HEADS * T
                            dst = qm[rows, o:o + HEADS * T].rearrange("p (g s q) -> p g s q", g=G, s=SLOTS)[:, g, :, :]
                            nc.gpsimd.tensor_tensor(dst, src, zero16[rows, :].unsqueeze(2).broadcast_to([32, SLOTS, T]), ALU.add)\
                              .then_inc(s.qm, 1)
                    for b in range(NB):
                        pool.wait_ge(s.rden, NB * i + b + 1)
                        nc.gpsimd.tensor_tensor(asb, asb, osb, ALU.mult).then_inc(s.a, 1)
                f = FF[a]
                with pool.Fori(0, BLOCKS) as i:
                    for e in range(EXPERTS):
                        hi = (hh, hh2)[e % 2]
                        if e < 2:
                            pool.wait_ge(f.mm2, ONE + EXPERTS * i)
                        else:
                            pool.wait_ge(f.mm2, ONE + EXPERTS * i + e - 1)
                        for c in range(HC):
                            w = slice(c * 512, c * 512 + 512)
                            pool.wait_ge(f.gelu, ONE + EXPERTS * HC * i + HC * e + c + 1)
                            nc.gpsimd.tensor_tensor(hi[:, w], h32[:, w], zero32[:].broadcast_to([P, 512]), ALU.add)\
                              .then_inc(f.high, 1)


def kernel(**inputs):
    import numpy as np
    import concourse.bacc as bacc
    from concourse.bass_utils import run_bass_kernel_spmd as run

    g = {k: np.asarray(v) for k, v in inputs.items()}

    def heads_rows(w):
        n = w.shape[1]
        r = w.reshape(SLOTS, G, DH, n)
        z = np.zeros((SLOTS, G, DH, n), w.dtype)
        return np.concatenate([r, r, r, z], axis=2).reshape(SLOTS, P, n).transpose(1, 0, 2)

    def weights(pre, last):
        q, k, v, p = (g[f"{pre}_W{n}"] for n in ("q", "k", "v", last))
        blocks = [heads_rows(q), heads_rows(k), v[:, None, :]]
        pc = p.T.reshape(SLOTS, G, DH, D)
        pc = np.concatenate([pc, np.zeros((SLOTS, G, 32 - DH, D), p.dtype)], axis=2)
        blocks.append(pc.reshape(SLOTS, P, D).transpose(2, 0, 1))
        return np.ascontiguousarray(np.concatenate(blocks, axis=1).reshape(P, BLK * P))

    def qk_bias(pre):
        q = heads_rows(g[f"{pre}_bq"][:, None])[:, :, 0]
        k = heads_rows(g[f"{pre}_bk"][:, None])[:, :, 0].copy()
        k[MROW::32, :] = MSCALE
        return np.ascontiguousarray(np.concatenate([q, k], axis=1))

    row = np.arange(P) % 32
    masks = np.stack([-((row >= 16) & (row < 24)).astype(np.float32), -((row >= 8) & (row < 16)).astype(np.float32)], 1)
    sel = (np.arange(P)[:, None] == (np.arange(P) // 32 * 32 + 8)[None, :]).astype(np.float32)
    rel = g["L0_attn_b_rel_emb"]
    rel = rel[np.clip(np.arange(REL) - (T - 1), -REL_MAX, REL_MAX) + REL_MAX].T
    rel = np.tile(np.concatenate([rel, rel, rel, np.zeros_like(rel)], axis=0), (G, 1))
    arrays = {
        "x": g["L0_attn_a_x"].reshape(TILES, P, D).transpose(1, 0, 2).reshape(P, NT),
        "wa": weights("L0_attn_a", "p"), "wb": weights("L0_attn_b", "o"),
        "bias_a": qk_bias("L0_attn_a"), "bias_b": qk_bias("L0_attn_b"),
        "bv_a": np.tile(g["L0_attn_a_bv"][None, :], (P, 1)), "bv_b": np.tile(g["L0_attn_b_bv"][None, :], (P, 1)),
        "bp_a": g["L0_attn_a_bp"][None, :], "bp_b": g["L0_attn_b_bo"][None, :],
        "rel": rel, "masks": masks, "ident": np.eye(P, dtype=np.float32), "sel": sel,
        "gate": g["L0_ffn_gate_weight"].T,
        "w1": g["L0_ffn_w1"].reshape(EXPERTS * HID, D).T,
        "b1": g["L0_ffn_b1"].reshape(EXPERTS * HC, P).T,
        "w2": g["L0_ffn_w2"].transpose(2, 0, 1).reshape(HC, P, EXPERTS, D).transpose(1, 2, 0, 3).reshape(P, EXPERTS * HID),
        "b2": g["L0_ffn_b2"],
    }
    nc = bacc.Bacc("TRN2", target_bir_lowering=False, num_devices=1)
    args = []
    for name in list(arrays):
        arrays[name] = np.ascontiguousarray(arrays[name])
        args.append(nc.dram_tensor(name, arrays[name].shape, F32, kind="ExternalInput").ap())
    args.append(nc.dram_tensor("out", (P, NT), F32, kind="ExternalOutput").ap())
    network(nc, *args)
    r = run(nc, [arrays], core_ids=[0])
    y = r.results[0]["out"]
    return np.ascontiguousarray(y.reshape(P, TILES, D).transpose(1, 0, 2).reshape(B, T, D))
```

```python
from contextlib import ExitStack

import concourse.bass as bass
from concourse import mybir

F32 = mybir.dt.float32
F16 = mybir.dt.float16
I32 = mybir.dt.int32
ALU = mybir.AluOpType
ACT = mybir.ActivationFunctionType
AX = mybir.AxisListType

P = 128
B, T, D = 16, 256, 128
NT = B * T
TILES = NT // P
HEADS, DH = 16, 8
G = 4
SLOTS = HEADS // G
KH = T // P
NB = 2
PAIRS = B // NB
GT = NB * T
QH = T // 2
QCOLS = NB * HEADS * QH
EXPERTS, HID = 8, 512
HC = HID // P
BLOCKS = NT // 512
GATED = 4 * 128 * 6
EPS = 1e-5
REL = 2 * T - 1
REL_MAX = 128
MROW = 24
MSCALE = 256.0
SCALE = float(DH) ** -0.5
ONE = 1
BLK = 10


class Setup:

    def __init__(self, sem):
        self.x = sem("x")
        self.consts = sem("consts")
        self.weights = sem("weights")
        self.alpha = sem("alpha")
        self.sign = sem("sign")
        self.binar = sem("binar")
        self.tr = sem("tr")
        self.evac = sem("evac")
        self.split = sem("split")
        self.ready = sem("ready")
        self.ones = sem("ones")


class LayerNorm:

    def __init__(self, sem):
        self.stats = sem("stats")
        self.col = sem("col")
        self.sqrt = sem("sqrt")
        self.rstd = sem("rstd")
        self.normed = sem("normed")
        self.high = sem("high")
        self.logit = sem("logit")
        self.low = sem("low")
        self.logit_out = sem("logit_out")
        self.tr = sem("tr")
        self.begun = [self.low, self.logit_out, self.tr]


class Attention:

    def __init__(self, sem):
        self.bias = sem("bias")
        self.proj = sem("proj")
        self.evac = sem("evac")
        self.t16 = sem("t16")
        self.split = sem("split")
        self.qm = sem("qm")
        self.v = sem("v")
        self.v_out = sem("v_out")
        self.e = sem("e")
        self.e_high = sem("e_high")
        self.e_low = sem("e_low")
        self.s1 = sem("s1")
        self.s1_used = sem("s1_used")
        self.r2 = sem("r2")
        self.rt = sem("rt")
        self.m3 = sem("m3")
        self.m3h = sem("m3h")
        self.m_row = sem("m_row")
        self.s2 = sem("s2")
        self.exp = sem("exp")
        self.pv = sem("pv")
        self.o_copy = sem("o_copy")
        self.ot = sem("ot")
        self.rden = sem("rden")
        self.a = sem("a")
        self.at = sem("at")
        self.at_copy = sem("at_copy")
        self.pp = sem("pp")
        self.x_new = sem("x_new")


class Threshold:

    def __init__(self, sem):
        self.cnt = sem("cnt")
        self.tot = sem("tot")
        self.step = sem("step")
        self.gate = sem("gate")


class Experts:

    def __init__(self, sem):
        self.raw = sem("raw")
        self.w_high = sem("w_high")
        self.w_low = sem("w_low")
        self.gst = sem("gst")
        self.gT = sem("gT")
        self.gTs = sem("gTs")
        self.b2 = sem("b2")
        self.mm1 = sem("mm1")
        self.high = sem("high")
        self.gelu = sem("gelu")
        self.gated = sem("gated")
        self.b2_used = sem("b2_used")
        self.mm2 = sem("mm2")
        self.low = sem("low")
        self.begun = [self.gelu, self.gated, self.b2_used, self.mm2, self.low]


def network(nc, x, wa, wb, bias_a, bias_b, bv_a, bv_b, bp_a, bp_b, rel, masks, ident, gate, w1, b1, w2, b2, out):
    with ExitStack() as ctx:
        def sb(name, shape, dt):
            return ctx.enter_context(nc.sbuf_tensor(name, shape, dt))

        xs = sb("xs", [P, NT], F32)
        xh = sb("xh", [P, NT], F16)
        xl = sb("xl", [P, NT], F16)
        lnv = sb("lnv", [P, 8, TILES], F32)
        ident32 = sb("ident32", [P, P], F32)
        ident16 = sb("ident16", [P, P], F16)
        ones16 = sb("ones16", [P, P], F16)
        mask = sb("mask", [P, 2], F32)
        wth = [sb(f"wth{n}", [P, 9 * P], F16) for n in "ab"]
        wtl = [sb(f"wtl{n}", [P, 9 * P], F16) for n in "ab"]
        wpt = [sb(f"wpt{n}", [P, P], F32) for n in "ab"]
        qkb = [sb(f"qkb{n}", [P, 2 * SLOTS], F32) for n in "ab"]
        bv = [sb(f"bv{n}", [P, P], F32) for n in "ab"]
        bp = [sb(f"bp{n}", [P, P], F32) for n in "ab"]
        zero32 = sb("zero32", [P, 1], F32)
        zero16 = sb("zero16", [P, 1], F16)
        alpha = sb("alpha", [P, BLK], F32)
        relh = sb("relh", [P, REL], F16)
        gth = sb("gth", [P, EXPERTS], F16)
        gtl = sb("gtl", [P, EXPERTS], F16)
        gt32 = sb("gt32", [P, EXPERTS], F32)
        b1s = sb("b1s", [P, EXPERTS * HC], F32)
        b2s = sb("b2s", [EXPERTS, D], F32)
        share = sb("share", [P, 16384], F16)
        w1h, w1l, w2h, w2l = (share[:, 4096 * n:4096 * n + 4096] for n in range(4))
        qm = [share[:, 8192 * n:8192 * n + 8192] for n in range(2)]
        ks = [sb(f"ks{n}", [P, SLOTS * GT], F16) for n in range(2)]
        qs = sb("qs", [P, SLOTS * GT], F16)
        x32 = sb("x32", [P, 4, 512], F32)
        t16 = sb("t16", [P, 2, 512], F16)
        vp = [sb(f"vp{n}", [P, NB * KH * HEADS * 32], F32) for n in range(2)]
        pt = sb("pt", [P, 4, KH * G * QH], F32)
        rmax = sb("rmax", [P, KH, P], F32)
        r2 = sb("r2", [P, P], F32)
        m3 = sb("m3", [P, 32], F32)
        m3h = sb("m3h", [P, 32], F16)
        osb = sb("osb", [P, SLOTS * QH], F32)
        rden = sb("rden", [P, HEADS], F32)
        asb = sb("asb", [P, P], F32)
        ats = sb("ats", [P, P], F32)
        lg = sb("lg", [P, TILES * EXPERTS], F32)
        cnt = sb("cnt", [P, 1], F16)
        tv = sb("tv", [P, 8], F32)
        ti = sb("ti", [P, 4], I32)
        big = sb("big", [P, 32768], F16)

        raw1 = big[:, 0:8192].bitcast(F32)
        raw2 = big[:, 8192:16384].bitcast(F32)
        rawa = big[:, 16384:16384 + 2 * BLK * P].bitcast(F32)
        rawb = big[:, 20480:20480 + 2 * BLK * P].bitcast(F32)
        sg = big[:, 27648:27648 + 2 * BLK * P].bitcast(F32)
        rawr = big[:, 24576:24576 + 2 * REL].bitcast(F32)
        tmp16 = big[:, 26624:26624 + 512]
        eh = [big[:, 8192 * n:8192 * n + 8192] for n in range(2)]
        el = [big[:, 16384 + 8192 * n:16384 + 8192 * n + 8192] for n in range(2)]
        h32 = big[:, 0:4096].bitcast(F32)
        hh = big[:, 4096:8192]
        hl = big[:, 8192:12288]
        hh2 = big[:, 12288:16384]
        hl2 = big[:, 16384:20480]
        gst = big[:, 20480:20544].bitcast(F32)
        gtt = big[0:EXPERTS, 20544:21568].bitcast(F32)
        xn = big[:, 28672:30720].bitcast(F32).rearrange("p (a b) -> p a b", a=2)
        stats = big[:, 30720:30720 + 12 * TILES].bitcast(F32).rearrange("p (t s) -> p t s", s=6)
        zt = big[:, 31232:31744].bitcast(F32)
        junk = big[:, 31744:32000]

        ps = ctx.enter_context(nc.psum_tensor("ps", [P, 8, 512], F32))

        def region(v):
            return ps[:, 2 + 2 * (v % 2):4 + 2 * (v % 2), :].rearrange("p a b -> p (a b)")

        def sem(phase):
            return lambda name: ctx.enter_context(nc.semaphore(f"{phase}_{name}"))

        su = Setup(sem("setup"))
        LN = [LayerNorm(sem(f"ln{n}")) for n in range(4)]
        AT = [Attention(sem(f"attn{n}")) for n in "ab"]
        TH = [Threshold(sem(f"thr{n}")) for n in range(2)]
        FF = [Experts(sem(f"ffn{n}")) for n in range(2)]
        out_done = ctx.enter_context(nc.semaphore("out_done"))

        block = ctx.enter_context(nc.Block())

        def heads(cols, b, slot):
            return cols.rearrange("p (g b s q) -> p g b s q", g=G, b=NB, s=SLOTS)[:, :, b, slot, :]

        def since(eng, sem, n):
            if not isinstance(n, int) or n > 0:
                eng.wait_ge(sem, n)

        @block.sync
        def _(sp):
            for n in range(4):
                sp.dma_start(xs[:, 1024 * n:1024 * n + 1024], x[:, 1024 * n:1024 * n + 1024]).then_inc(su.x, 16)
            for dst, src in ((ident32, ident), (mask, masks), (qkb[0], bias_a), (qkb[1], bias_b), (bv[0], bv_a),
                             (bv[1], bv_b), (bp[0], bp_a), (bp[1], bp_b), (gt32, gate), (b1s, b1), (b2s, b2)):
                sp.dma_start(dst[:], src).then_inc(su.consts, 16)
            for dst, src in ((rawa, wa), (rawb, wb), (rawr, rel)):
                sp.dma_start(dst, src).then_inc(su.weights, 16)
            for s in (*LN, *FF):
                for sem in s.begun:
                    sp.sem_inc(sem, ONE)
            for a in range(2):
                s = AT[a]
                if a == 0:
                    for dst, src in ((raw1, w1), (raw2, w2)):
                        sp.dma_start(dst, src).then_inc(FF[0].raw, 16)
                with sp.Fori(0, PAIRS // 2) as i:
                    for k in range(4):
                        sp.wait_ge(s.m3h, 4 * i + k + 1)
                        for g in range(G):
                            o = (k % 2) * QCOLS + g * QCOLS // G
                            dst = qm[k // 2][32 * g + MROW:32 * g + MROW + 1, o:o + QCOLS // G]
                            sp.dma_start(dst.rearrange("p (k q) -> p k q", q=32), m3h[32 * g:32 * g + 32, :])\
                              .then_inc(s.m_row, 16)
                if a == 1:
                    sp.wait_ge(s.s2, 16 * PAIRS)
                    for dst, src in ((raw1, w1), (raw2, w2)):
                        sp.dma_start(dst, src).then_inc(FF[1].raw, 16)
            sp.wait_ge(FF[1].gated, ONE + BLOCKS * EXPERTS)
            for n in range(4):
                sp.dma_start(out[:, 1024 * n:1024 * n + 1024], xs[:, 1024 * n:1024 * n + 1024]).then_inc(out_done, 16)
            sp.wait_ge(out_done, 64)

        def ahead_of(v, part, kinds, rel_on):
            if v >= 6:
                return kinds[len(kinds) * (v - 6) // 2:len(kinds) * (v - 5) // 2] if part else []
            work = [(1, k) for k in range(16)] * rel_on + [(2, k) for k in range(16)]
            n, c = len(work), 2 * v + part
            return work[n * c // 12:n * (c + 1) // 12] + [(3, 0)] * (c == 11)

        QUERIES = [(0, k) for k in range(4)]
        KEYS_VALUES = [(0, k) for k in range(4, 10)]

        def pe_setup(pe):
            pe.wait_ge(su.consts, 176)
            pe.wait_ge(su.weights, 48)
            for k in range(2 * BLK):
                raw = rawa if k < BLK else rawb
                if k == 0:
                    pe.wait_ge(su.binar, 1)
                if k >= 2:
                    pe.wait_ge(su.evac, k - 1)
                kk = k % BLK
                nc.tensor.transpose(ps[:, k % 2, 0:P], raw[:, kk * P:kk * P + P], ident32[:]).then_inc(su.tr, 1)

        def pe_ln(pe, s, logits, first):
            with pe.Fori(0, 4) as i:
                for j in range(2):
                    pe.wait_ge(s.normed, 2 * i + j + 1)
                    if j == 0:
                        pe.wait_ge(s.low, ONE + 2 * i)
                    else:
                        pe.wait_ge(s.low, ONE + 2 * i)
                    for t in range(4):
                        m = nc.tensor.transpose(ps[:, j, t * P:t * P + P], xn[:, j, t * P:t * P + P], ident32[:])
                    m.then_inc(s.tr, 1)
                    if logits:
                        pe.wait_ge(s.low, ONE + 2 * i + j + 1)
                        pe.wait_ge(s.logit_out, ONE + 2 * i)
                        for t in range(4):
                            c = (i * 8 + j * 4 + t) * P
                            o = ps[:, 2 + j, t * EXPERTS:(t + 1) * EXPERTS]
                            nc.tensor.matmul(o, xh[:, bass.ds(c, P)], gth[:], start=True, stop=False)
                            nc.tensor.matmul(o, xh[:, bass.ds(c, P)], gtl[:], start=False, stop=False)
                            m = nc.tensor.matmul(o, xl[:, bass.ds(c, P)], gth[:], start=False, stop=True)
                        m.then_inc(s.logit, 1)

        def pe_attn(pe, a):
            s = AT[a]
            rel_on = a == 1

            def prep(k, p, par):
                if k < 8:
                    if k in (0, 1):
                        if isinstance(p, int) and p == 1:
                            pe.wait_ge(s.v_out, TILES // B * 2)
                        else:
                            since(pe, s.m3, 2 * p - 1)
                    elif k in (4, 5):
                        since(pe, s.m3, 2 * p)
                    if k >= 2:
                        pe.wait_ge(s.evac, 8 * p + k - 1)
                    tok = bass.ds(p * GT, GT)
                    o = ps[:, k % 2, :]
                    w = slice(k * P, k * P + P)
                    nc.tensor.matmul(o, wth[a][:, w], xh[:, tok], start=True, stop=False)
                    nc.tensor.matmul(o, wth[a][:, w], xl[:, tok], start=False, stop=False)
                    nc.tensor.matmul(o, wtl[a][:, w], xh[:, tok], start=False, stop=True).then_inc(s.proj, 1)
                else:
                    pe.wait_ge(s.evac, 8 * p + k - 1)
                    for j in range(2):
                        tok = bass.ds(p * GT + (2 * (k - 8) + j) * P, P)
                        o = ps[:, k % 2, j * P:j * P + P]
                        w = slice(8 * P, 9 * P)
                        nc.tensor.matmul(o, xh[:, tok], wth[a][:, w], start=True, stop=False)
                        nc.tensor.matmul(o, xh[:, tok], wtl[a][:, w], start=False, stop=False)
                        m = nc.tensor.matmul(o, xl[:, tok], wth[a][:, w], start=False, stop=True)
                    m.then_inc(s.v, 1)

            def banks_free(p, qh):
                if qh or isinstance(p, int) and p == 0:
                    pe.wait_ge(s.evac, 8 * PAIRS if isinstance(p, int) and p == PAIRS - 1 else 8 * p + 12)
                else:
                    pe.wait_ge(s.v_out, 4 * (p + 1))

            def relative(u, t, p, par, qh):
                kh, qc = u // 8, u % 8
                if u < 2:
                    banks_free(p, qh)
                else:
                    pe.wait_ge(s.e_low, 16 * t + u - 1)
                if u == 0:
                    pe.wait_ge(s.qm, 8 * (p + 1))
                cols = qm[par][:, qh * QCOLS:(qh + 1) * QCOLS]
                for j in range(16):
                    q = qc * 16 + j
                    w0 = T - 1 - (qh * QH + q) + kh * P
                    m = nc.tensor.matmul(ps[:, u % 2, j * 32:j * 32 + 32], relh[:, w0:w0 + P],
                                         cols[:, q:q + (NB * HEADS - 1) * QH + 1:QH], start=True, stop=True)
                m.then_inc(s.e, 1)

            def scores(o, b, slot, kh, par, qh, low):
                o = o.rearrange("p (g q) -> p g q", g=G)
                kcol = slot * GT + b * T + kh * P
                m = nc.tensor.matmul(o, ks[par][:, kcol:kcol + P],
                                     heads(qm[par][:, qh * QCOLS:(qh + 1) * QCOLS], b, slot), start=True, stop=not rel_on)
                if rel_on:
                    e = slice(kh * QCOLS, (kh + 1) * QCOLS)
                    m = nc.tensor.matmul(o, ident16[:], heads(eh[qh][:, e], b, slot), start=False, stop=not low)
                    if low:
                        m = nc.tensor.matmul(o, ident16[:], heads(el[qh][:, e], b, slot), start=False, stop=True)
                return m

            def first_pass(w, t, p, par, qh):
                b, slot, kh = w // 8, w // 2 % 4, w % 2
                if w < 2:
                    if rel_on:
                        pe.wait_ge(s.e_low, 16 * (t + 1))
                    else:
                        banks_free(p, qh)
                else:
                    pe.wait_ge(s.s1_used, 16 * t + w - 1)
                if w == 0:
                    pe.wait_ge(s.split, 8 * (p + 1))
                    pe.wait_ge(s.qm, 8 * (p + 1))
                scores(ps[:, w % 2, :], b, slot, kh, par, qh, False).then_inc(s.s1, 1)

            def max_transpose(t):
                pe.wait_ge(s.r2, t + 1)
                nc.tensor.transpose(ps[:, 0, 0:P], r2[:], ident32[:]).then_inc(s.rt, 1)

            def second_pass(v, t, par, qh):
                b, slot = v // 4, v % 4
                since(pe, s.exp, 8 * t + v - 1)
                if v == 0:
                    pe.wait_ge(s.m_row, 64 * (t + 1))
                for kh in range(KH):
                    m = scores(region(v)[:, 512 * kh:512 * kh + 512], b, slot, kh, par, qh, True)
                m.then_inc(s.s2, 1)

            def pv(v, t, p, par):
                b, slot = v // 4, v % 4
                pe.wait_ge(s.exp, 8 * t + v + 1)
                if slot == 0:
                    since(pe, s.o_copy, 2 * t + b)
                    pe.wait_ge(s.v_out, 4 * (p + 1))
                for kh in range(KH):
                    for g in range(G):
                        v0 = ((b * KH + kh) * HEADS + slot * G + g) * 32
                        m = nc.tensor.matmul(ps[32 * g:32 * g + 32, 6, slot * QH:slot * QH + QH], vp[par][:, v0:v0 + 32],
                                             pt[:, v % 4, (kh * G + g) * QH:(kh * G + g + 1) * QH], start=kh == 0,
                                             stop=kh == KH - 1, tile_position=(0, 32 * g))
                m.then_inc(s.pv, 1)

            def out_transpose(n):
                pe.wait_ge(s.o_copy, n + 1)
                since(pe, s.x_new, n)
                for slot in range(SLOTS):
                    m = nc.tensor.transpose(ps[:, 7, slot * QH:slot * QH + QH], osb[:, slot * QH:slot * QH + QH],
                                            ident32[:])
                m.then_inc(s.ot, 1)

            def back_transpose(n):
                pe.wait_ge(s.a, n + 1)
                nc.tensor.transpose(ps[:, 7, 0:P], asb[:], ident32[:]).then_inc(s.at, 1)

            def project(n):
                pe.wait_ge(s.at_copy, n + 1)
                nc.tensor.matmul(ps[:, 7, 0:P], ats[:], wpt[a][:], start=True, stop=True).then_inc(s.pp, 1)

            def step(p, par, qh, projections, first=False, ahead=True):
                t = 2 * p + qh
                pn, parn, qn = (p, par, 1) if qh == 0 else (p + 1, 1 - par, 0)
                for v in range(8):
                    second_pass(v, t, par, qh)
                    for part in range(2):
                        if part == 0 and not first:
                            if v == 0:
                                pv(7, t - 1, p if qh else p - 1, par if qh else 1 - par)
                            if v == 1:
                                out_transpose(2 * t - 1)
                            if v == 2:
                                back_transpose(2 * t - 1)
                            if v == 3:
                                project(2 * t - 1)
                        if part == 0 and v == 5:
                            out_transpose(2 * t)
                        if part == 1 and v:
                            pv(v - 1, t, p, par)
                        if part == 1 and v == 6:
                            back_transpose(2 * t)
                        if part == 1 and v == 7:
                            project(2 * t)
                        for kind, k in ahead_of(v, part, projections, rel_on) if ahead else []:
                            if kind == 0:
                                prep(k, p + 1 + qh, par if qh else 1 - par)
                            elif kind == 1:
                                relative(k, t + 1, pn, parn, qn)
                            elif kind == 2:
                                first_pass(k, t + 1, pn, parn, qn)
                            else:
                                max_transpose(t + 1)

            pe.wait_ge(LN[2 * a].low, ONE + 8)
            for k in range(10):
                prep(k, 0, 0)
            for k in range(4):
                prep(k, 1, 1)
            if rel_on:
                for u in range(16):
                    relative(u, 0, 0, 0, 0)
            for w in range(16):
                first_pass(w, 0, 0, 0, 0)
            max_transpose(0)
            step(0, 0, 0, KEYS_VALUES, first=True)
            with pe.Fori(0, PAIRS // 2 - 1) as i:
                for par in range(2):
                    step(2 * i + par, par, 1, QUERIES)
                    step(2 * i + par + 1, 1 - par, 0, KEYS_VALUES)
            last = PAIRS - 2
            step(last, 0, 1, [])
            step(last + 1, 1, 0, [])
            step(last + 1, 1, 1, [], ahead=False)
            t = 2 * PAIRS - 1
            pv(7, t, last + 1, 1)
            out_transpose(2 * t + 1)
            back_transpose(2 * t + 1)
            project(2 * t + 1)

        def pe_threshold(pe, s):
            with pe.Fori(0, 32) as i:
                pe.wait_ge(s.cnt, i + 1)
                nc.tensor.matmul(ps[:, 6, 0:1], ones16[:], cnt[:], start=True, stop=True).then_inc(s.tot, 1)

        def pe_ffn(pe, s, ln):
            def up(i, e):
                for c in range(HC):
                    n = EXPERTS * HC * i + HC * e + c
                    if e:
                        pe.wait_ge(s.gelu, ONE + n - HC + 1)
                    else:
                        pe.wait_ge(s.gelu, ONE + EXPERTS * HC * i)
                    w = slice(e * HID + c * P, e * HID + c * P + P)
                    tok = bass.ds(i * 512, 512)
                    nc.tensor.matmul(ps[:, c, :], w1h[:, w], xh[:, tok], start=True, stop=False)
                    nc.tensor.matmul(ps[:, c, :], w1h[:, w], xl[:, tok], start=False, stop=False)
                    nc.tensor.matmul(ps[:, c, :], w1l[:, w], xh[:, tok], start=False, stop=True).then_inc(s.mm1, 1)

            def down(i, e):
                hi, lo = ((hh, hl), (hh2, hl2))[e % 2]
                pe.wait_ge(s.low, ONE + HC * (EXPERTS * i + e + 1))
                pe.wait_ge(s.high, HC * (EXPERTS * i + e + 1))
                if e >= 2:
                    pe.wait_ge(s.gated, ONE + EXPERTS * i + e - 1)
                else:
                    pe.wait_ge(s.gated, ONE + EXPERTS * i)
                for t in range(4):
                    for c in range(HC):
                        h = slice(c * 512 + t * P, c * 512 + t * P + P)
                        w = slice((e * HC + c) * P, (e * HC + c + 1) * P)
                        o = ps[:, 4 + e % 2, t * P:t * P + P]
                        nc.tensor.matmul(o, hi[:, h], w2h[:, w], start=c == 0, stop=False)
                        nc.tensor.matmul(o, hi[:, h], w2l[:, w], start=False, stop=False)
                        m = nc.tensor.matmul(o, lo[:, h], w2h[:, w], start=False, stop=c == HC - 1)
                m.then_inc(s.mm2, 1)

            pe.wait_ge(ln.low, ONE + 8)
            pe.wait_ge(ln.logit_out, ONE + 8)
            pe.wait_ge(s.w_high, 2)
            pe.wait_ge(s.w_low, 2)
            with pe.Fori(0, BLOCKS) as i:
                up(i, 0)
                pe.wait_ge(s.gst, i + 1)
                pe.wait_ge(s.b2_used, ONE + i)
                for t in range(4):
                    m = nc.tensor.transpose(ps[0:EXPERTS, 6, t * P:t * P + P], gst[:, t * EXPERTS:(t + 1) * EXPERTS],
                                            ident32[:])
                m.then_inc(s.gT, 1)
                for e in range(1, EXPERTS):
                    up(i, e)
                    if e == 1:
                        pe.wait_ge(s.gTs, i + 1)
                        for t in range(4):
                            m = nc.tensor.matmul(ps[:, 7, t * P:t * P + P], gtt[:, t * P:t * P + P], b2s[:],
                                                 start=True, stop=True)
                        m.then_inc(s.b2, 1)
                    down(i, e - 1)
                down(i, EXPERTS - 1)

        @block.tensor
        def _(pe):
            pe_setup(pe)
            pe.wait_ge(su.evac, 2 * BLK)
            pe.wait_ge(su.split, 1)
            pe_ln(pe, LN[0], False, True)
            pe_attn(pe, 0)
            pe_ln(pe, LN[1], True, False)
            pe_threshold(pe, TH[0])
            pe_ffn(pe, FF[0], LN[1])
            pe_ln(pe, LN[2], False, False)
            pe_attn(pe, 1)
            pe_ln(pe, LN[3], True, False)
            pe_threshold(pe, TH[1])
            pe_ffn(pe, FF[1], LN[3])

        def act_ln(act, s):
            act.wait_ge(s.col, 1)
            nc.scalar.activation(lnv[:, 3, :], lnv[:, 2, :], ACT.Sqrt).then_inc(s.sqrt, 1)
            with act.Fori(0, 4) as i:
                for j in range(2):
                    act.wait_ge(s.tr, ONE + 2 * i + j + 1)
                    nc.scalar.activation(xh[:, bass.ds(i * 1024 + j * 512, 512)], ps[:, j, :], ACT.Copy)\
                      .then_inc(s.high, 1)

        def act_attn(act, a):
            s = AT[a]
            rel_on = a == 1

            def evacuate(k, p):
                if k >= 8:
                    return
                act.wait_ge(s.proj, 8 * p + k + 1)
                since(act, s.split, 8 * p + k - 3)
                nc.scalar.activation(x32[:, k % 4, :], ps[:, k % 2, :], ACT.Identity, bias=qkb[a][:, k:k + 1])\
                  .then_inc(s.evac, 1)

            def relative_high(u, t, qh):
                kh, qc = u // 8, u % 8
                act.wait_ge(s.e, 16 * t + u + 1)
                if u == 0:
                    since(act, s.s2, 8 * (t - 1))
                src = ps[:, u % 2, :].rearrange("p (q n) -> p n q", q=16)
                dst = eh[qh][:, kh * QCOLS:(kh + 1) * QCOLS].rearrange("p (n q) -> p n q", q=QH)[
                    :, :, qc * 16:qc * 16 + 16]
                nc.scalar.activation(dst, src, ACT.Copy).then_inc(s.e_high, 1)

            def exponential(v, t):
                act.wait_ge(s.s2, 8 * t + v + 1)
                since(act, s.pv, 8 * t + v - 3)
                nc.scalar.activation(pt[:, v % 4, :], region(v), ACT.Exp, scale=SCALE).then_inc(s.exp, 1)

            def out_copy(n):
                act.wait_ge(s.pv, 4 * (n + 1))
                since(act, s.ot, n)
                nc.scalar.activation(osb[:], ps[:, 6, :], ACT.Copy).then_inc(s.o_copy, 1)

            def back_copy(n):
                act.wait_ge(s.at, n + 1)
                nc.scalar.activation(ats[:], ps[:, 7, 0:P], ACT.Copy).then_inc(s.at_copy, 1)

            def step(p, par, qh, projections, first=False, ahead=True):
                t = 2 * p + qh
                for v in range(8):
                    exponential(v, t)
                    if not first:
                        if v == 0:
                            out_copy(2 * t - 1)
                        if v == 2:
                            back_copy(2 * t - 1)
                    for part in range(2):
                        if part == 1 and v == 4:
                            out_copy(2 * t)
                        if part == 1 and v == 6:
                            back_copy(2 * t)
                        for kind, k in ahead_of(v, part, projections, rel_on) if ahead else []:
                            if kind == 0:
                                evacuate(k, p + 1 + qh)
                            elif kind == 1:
                                relative_high(k, t + 1, 1 - qh)

            for k in range(8):
                evacuate(k, 0)
            for k in range(4):
                evacuate(k, 1)
            if rel_on:
                for u in range(16):
                    relative_high(u, 0, 0)
            step(0, 0, 0, KEYS_VALUES, first=True)
            with act.Fori(0, PAIRS // 2 - 1) as i:
                for par in range(2):
                    step(2 * i + par, par, 1, QUERIES)
                    step(2 * i + par + 1, 1 - par, 0, KEYS_VALUES)
            last = PAIRS - 2
            step(last, 0, 1, [])
            step(last + 1, 1, 0, [])
            step(last + 1, 1, 1, [], ahead=False)
            out_copy(4 * PAIRS - 1)
            back_copy(4 * PAIRS - 1)

        def act_ffn(act, s):
            with act.Fori(0, BLOCKS) as i:
                for e in range(EXPERTS):
                    for c in range(HC):
                        n = EXPERTS * HC * i + HC * e + c
                        act.wait_ge(s.mm1, n + 1)
                        if e:
                            act.wait_ge(s.low, ONE + n - HC + 1)
                        else:
                            act.wait_ge(s.low, ONE + EXPERTS * HC * i)
                        nc.scalar.activation(h32[:, c * 512:c * 512 + 512], ps[:, c, :], ACT.Gelu_apprx_tanh,
                                             bias=b1s[:, e * HC + c:e * HC + c + 1]).then_inc(s.gelu, 1)

        @block.scalar
        def _(act):
            act.wait_ge(su.weights, 48)
            act.wait_ge(su.ones, 5)
            nc.scalar.activation(sg, rawa, ACT.Sign).then_inc(su.sign, 1)
            for n in range(4):
                if n % 2:
                    act.wait_ge(FF[n // 2].raw, 32)
                    act.wait_ge(AT[n // 2].s2, 16 * PAIRS)
                    nc.scalar.activation(w1h, raw1, ACT.Copy).then_inc(FF[n // 2].w_high, 1)
                    nc.scalar.activation(w2h, raw2, ACT.Copy).then_inc(FF[n // 2].w_high, 1)
                act_ln(act, LN[n])
                if n % 2 == 0:
                    act_attn(act, n // 2)
                else:
                    act_ffn(act, FF[n // 2])

        def dve_setup(v):
            nc.vector.memset(vp[0][:], 0.0).then_inc(su.ones, 1)
            nc.vector.memset(vp[1][:], 0.0).then_inc(su.ones, 1)
            nc.vector.memset(ones16[:], 1.0).then_inc(su.ones, 1)
            v.wait_ge(su.ones, 3)
            for n in range(2):
                nc.vector.memset(vp[n][:].rearrange("p (n c) -> p n c", c=32)[:, :, 8:9], 1.0).then_inc(su.ones, 1)
            v.wait_ge(su.weights, 48)
            v.wait_ge(su.consts, 176)
            nc.vector.tensor_copy(ident16[:], ident32[:]).then_inc(su.alpha, 1)
            nc.vector.tensor_reduce(alpha[:], rawa.rearrange("p (n c) -> p n c", c=P), AX.X, ALU.add,
                                    apply_absolute_value=True).then_inc(su.alpha, 1)
            v.wait_ge(su.alpha, 2)
            nc.vector.tensor_scalar(alpha[:], alpha[:], 1.0 / D, None, ALU.mult).then_inc(su.alpha, 1)
            v.wait_ge(su.sign, 1)
            v.wait_ge(su.alpha, 3)
            nc.vector.tensor_tensor(sg, sg, rawa, ALU.subtract).then_inc(su.alpha, 1)
            v.wait_ge(su.alpha, 4)
            nc.vector.tensor_tensor(rawa, rawa, sg, ALU.add).then_inc(su.alpha, 1)
            v.wait_ge(su.alpha, 5)
            blocks = rawa.rearrange("p (n c) -> p n c", c=P)
            nc.vector.tensor_tensor(blocks, blocks, alpha[:].unsqueeze(2).broadcast_to([P, BLK, P]), ALU.mult)\
              .then_inc(su.binar, 1)
            for k in range(2 * BLK):
                a, kk = k // BLK, k % BLK
                v.wait_ge(su.tr, k + 1)
                src = ps[:, k % 2, 0:P]
                if kk < 9:
                    w = slice(kk * P, kk * P + P)
                    nc.vector.tensor_copy(wth[a][:, w], src).then_inc(su.alpha, 1)
                    v.wait_ge(su.alpha, 6 + 9 * a + kk)
                    nc.vector.tensor_tensor(wtl[a][:, w], src, wth[a][:, w], ALU.subtract).then_inc(su.evac, 1)
                else:
                    nc.vector.tensor_copy(wpt[a][:], src).then_inc(su.evac, 1)
            n = 5 + 18
            for hi, lo, raw in ((gth, gtl, gt32[:]),):
                nc.vector.tensor_copy(hi[:], raw).then_inc(su.alpha, 1)
                n += 1
                v.wait_ge(su.alpha, n)
                nc.vector.tensor_tensor(lo[:], raw, hi[:], ALU.subtract).then_inc(su.alpha, 1)
                n += 1
            nc.vector.tensor_copy(tmp16[:, 0:REL], rawr).then_inc(su.alpha, 1)
            n += 1
            v.wait_ge(su.alpha, n)
            nc.vector.scalar_tensor_tensor(out=relh[:], in0=tmp16[:, 0:REL], scalar=mask[:, 1:2], in1=rawr,
                                           op0=ALU.mult, op1=ALU.add).then_inc(su.split, 1)

        def dve_ln(v, s, logits):
            with v.Fori(0, 4) as i:
                for j in range(8):
                    m = nc.vector.bn_stats(stats[:, bass.ds(i * 8 + j, 1), :].rearrange("p a b -> p (a b)"),
                                           xs[:, bass.ds((i * 8 + j) * P, P)])
                    m.then_inc(s.stats, 1)
            v.wait_ge(s.stats, TILES)
            n = [0]

            def link(m):
                n[0] += 1
                m.then_inc(s.rstd, 1)
                v.wait_ge(s.rstd, n[0])

            me, ve, mo, vo = (stats[:, :, k] for k in (1, 2, 4, 5))
            c = [lnv[:, k, :] for k in range(8)]
            link(nc.vector.tensor_tensor(c[0], me, mo, ALU.add))
            link(nc.vector.tensor_tensor(c[1], me, mo, ALU.subtract))
            link(nc.vector.tensor_tensor(c[4], ve, vo, ALU.add))
            link(nc.vector.tensor_scalar(c[0], c[0], 0.5, None, ALU.mult))
            link(nc.vector.tensor_tensor(c[1], c[1], c[1], ALU.mult))
            link(nc.vector.tensor_scalar(c[4], c[4], 1.0 / D, EPS, ALU.mult, ALU.add))
            nc.vector.scalar_tensor_tensor(out=c[2], in0=c[1], scalar=0.25, in1=c[4], op0=ALU.mult, op1=ALU.add)\
              .then_inc(s.col, 1)
            v.wait_ge(s.sqrt, 1)
            link(nc.vector.reciprocal(c[5], c[3]))
            v.wait_ge(s.col, 1)
            link(nc.vector.tensor_tensor(c[6], c[5], c[5], ALU.mult))
            link(nc.vector.tensor_tensor(c[6], c[6], c[2], ALU.mult))
            link(nc.vector.tensor_scalar(c[6], c[6], -0.5, 1.5, ALU.mult, ALU.add))
            link(nc.vector.tensor_tensor(c[7], c[6], c[5], ALU.mult))
            with v.Fori(0, 4) as i:
                for j in range(2):
                    v.wait_ge(s.tr, ONE + 2 * i)
                    for t in range(4):
                        k = i * 8 + j * 4 + t
                        m = nc.vector.tensor_scalar(xn[:, j, t * P:t * P + P], xs[:, bass.ds(k * P, P)],
                                                    lnv[:, 0, bass.ds(k, 1)], lnv[:, 7, bass.ds(k, 1)],
                                                    ALU.subtract, ALU.mult)
                    m.then_inc(s.normed, 1)
                for j in range(2):
                    v.wait_ge(s.high, 2 * i + j + 1)
                    c0 = i * 1024 + j * 512
                    nc.vector.tensor_tensor(xl[:, bass.ds(c0, 512)], ps[:, j, :], xh[:, bass.ds(c0, 512)],
                                            ALU.subtract).then_inc(s.low, 1)
                if logits:
                    for j in range(2):
                        v.wait_ge(s.logit, 2 * i + j + 1)
                        nc.vector.tensor_copy(lg[:, bass.ds((i * 2 + j) * 32, 32)], ps[:, 2 + j, 0:32])\
                          .then_inc(s.logit_out, 1)

        def dve_attn(v, a):
            s = AT[a]
            rel_on = a == 1

            def prep(k, p, par):
                if k < 8:
                    if k == 0:
                        since(v, s.qm, 8 * p)
                    if k == 4:
                        since(v, s.s2, 16 * (p - 1))
                    v.wait_ge(s.evac, 8 * p + k + 1)
                    nc.vector.tensor_copy(t16[:, k % 2, :], x32[:, k % 4, :]).then_inc(s.t16, 1)
                    dst, c = (qs, 0) if k < SLOTS else (ks[par], 1)
                    v.wait_ge(s.t16, 8 * p + k + 1)
                    nc.vector.scalar_tensor_tensor(out=dst[:, (k % SLOTS) * GT:(k % SLOTS + 1) * GT],
                                                   in0=t16[:, k % 2, :], scalar=mask[:, c:c + 1], in1=x32[:, k % 4, :],
                                                   op0=ALU.mult, op1=ALU.add).then_inc(s.split, 1)
                else:
                    v.wait_ge(s.v, 2 * p + k - 7)
                    if k == 8:
                        since(v, s.pv, 16 * (p - 1))
                    for j in range(2):
                        t = 2 * (k - 8) + j
                        nc.vector.tensor_tensor(
                            vp[par][:, t * 512:t * 512 + 512].rearrange("p (n c) -> p n c", c=32)[:, :, 0:DH],
                            ps[:, k % 2, j * P:j * P + P].rearrange("p (n c) -> p n c", c=DH),
                            bv[a][:].rearrange("p (n c) -> p n c", c=DH), ALU.add).then_inc(s.v_out, 1)

            def relative_low(u, t, qh):
                kh, qc = u // 8, u % 8
                v.wait_ge(s.e_high, 16 * t + u + 1)
                src = ps[:, u % 2, :].rearrange("p (q n) -> p n q", q=16)
                hi, lo = (e[qh][:, kh * QCOLS:(kh + 1) * QCOLS].rearrange("p (n q) -> p n q", q=QH)[
                    :, :, qc * 16:qc * 16 + 16] for e in (eh, el))
                nc.vector.tensor_tensor(lo, src, hi, ALU.subtract).then_inc(s.e_low, 1)

            def reduce(w, t):
                b, slot, kh = w // 8, w // 2 % 4, w % 2
                v.wait_ge(s.s1, 16 * t + w + 1)
                dst = rmax[:, kh, :].rearrange("p (g b s q) -> p g b s q", g=G, b=NB, s=SLOTS)[:, :, b, slot, :]
                nc.vector.tensor_reduce(dst, ps[:, w % 2, :].rearrange("p (g q k) -> p g q k", g=G, k=32), AX.X, ALU.max,
                                        apply_transpose=True).then_inc(s.s1_used, 1)
                if w == 15:
                    v.wait_ge(s.s1_used, 16 * (t + 1))
                    nc.vector.tensor_tensor(r2[:], rmax[:, 0, :], rmax[:, 1, :], ALU.max).then_inc(s.r2, 1)

            def maxima(t):
                v.wait_ge(s.rt, t + 1)
                nc.vector.tensor_reduce(m3[:], ps[:, 0, 0:P].rearrange("p (k q) -> p q k", k=4), AX.X, ALU.max)\
                  .then_inc(s.m3, 1)
                v.wait_ge(s.m3, t + 1)
                nc.vector.tensor_scalar(m3h[:], m3[:], -1.0 / MSCALE, None, ALU.mult).then_inc(s.m3h, 1)

            def normalise(n):
                v.wait_ge(s.ot, n + 1)
                o = ps[:, 7, :].rearrange("p (h c) -> p h c", c=32)
                nc.vector.reciprocal(rden[:].unsqueeze(2), o[:, :, DH:DH + 1]).then_inc(s.rden, 1)
                v.wait_ge(s.rden, n + 1)
                nc.vector.tensor_tensor(asb[:].rearrange("p (h c) -> p h c", c=DH), o[:, :, 0:DH],
                                        rden[:].unsqueeze(2).broadcast_to([P, HEADS, DH]), ALU.mult).then_inc(s.a, 1)

            def residual(n, tile):
                v.wait_ge(s.pp, n + 1)
                xc = xs[:, bass.ds(tile * P, P)]
                nc.vector.tensor_tensor(xc, xc, ps[:, 7, 0:P], ALU.add).then_inc(s.x_new, 1)

            def step(p, par, qh, projections, first=False, ahead=True):
                t = 2 * p + qh
                for c in range(8):
                    if not first:
                        if c == 1:
                            normalise(2 * t - 1)
                        if c == 3:
                            residual(2 * t - 1, 4 * (p if qh else p - 1) + 2 + (1 - qh))
                    if c == 5:
                        normalise(2 * t)
                    for part in range(2):
                        for kind, k in ahead_of(c, part, projections, rel_on) if ahead else []:
                            if kind == 0:
                                prep(k, p + 1 + qh, par if qh else 1 - par)
                            elif kind == 1:
                                relative_low(k, t + 1, 1 - qh)
                            elif kind == 2:
                                reduce(k, t + 1)
                            else:
                                maxima(t + 1)
                    if c == 7:
                        residual(2 * t, 4 * p + qh)

            v.wait_ge(s.bias, 4)
            for k in range(10):
                prep(k, 0, 0)
            for k in range(4):
                prep(k, 1, 1)
            if rel_on:
                for u in range(16):
                    relative_low(u, 0, 0)
            for w in range(16):
                reduce(w, 0)
            maxima(0)
            step(0, 0, 0, KEYS_VALUES, first=True)
            with v.Fori(0, PAIRS // 2 - 1) as i:
                for par in range(2):
                    step(2 * i + par, par, 1, QUERIES)
                    step(2 * i + par + 1, 1 - par, 0, KEYS_VALUES)
            last = PAIRS - 2
            step(last, 0, 1, [])
            step(last + 1, 1, 0, [])
            step(last + 1, 1, 1, [], ahead=False)
            normalise(4 * PAIRS - 1)
            residual(4 * PAIRS - 1, 4 * PAIRS - 1)

        def dve_threshold(v, s):
            n = [0]

            def link(m):
                n[0] += 1
                m.then_inc(s.step, 1)
                v.wait_ge(s.step, n[0])

            neg, sgn, need, bitf, unit = (tv[:, k:k + 1] for k in range(5))
            kth = tv[:, 5:6]
            have, got, nxt, cand = (ti[:, k:k + 1] for k in range(4))
            total = NT * EXPERTS
            nc.vector.tensor_scalar(junk, lg[:], 0.0, 0.0, ALU.is_lt, ALU.add, accum_out=cnt[:]).then_inc(s.cnt, 1)
            v.wait_ge(s.tot, 1)
            link(nc.vector.tensor_scalar(neg, ps[:, 6, 0:1], float(GATED), None, ALU.is_ge))
            link(nc.vector.tensor_scalar(sgn, neg, -2.0, 1.0, ALU.mult, ALU.add))
            link(nc.vector.tensor_scalar(need, neg, float(2 * GATED - total - 1), float(total - GATED + 1),
                                         ALU.mult, ALU.add))
            link(nc.vector.tensor_scalar(zt, lg[:], sgn, None, ALU.mult))
            link(nc.vector.memset(have, 0))
            link(nc.vector.memset(bitf, float(2 ** 30)))
            link(nc.vector.tensor_copy(cand, bitf))
            base = n[0]
            with v.Fori(0, 31) as i:
                v.wait_ge(s.step, base + 5 * i)
                nc.vector.tensor_scalar(junk, zt, cand.bitcast(F32), 0.0, ALU.is_ge, ALU.add,
                                        accum_out=cnt[:]).then_inc(s.cnt, 1)
                v.wait_ge(s.cnt, i + 2)
                nc.vector.tensor_scalar(nxt, bitf, 0.5, None, ALU.mult).then_inc(s.step, 1)
                v.wait_ge(s.tot, i + 2)
                nc.vector.tensor_scalar(got, ps[:, 6, 0:1], need, bitf, ALU.is_ge, ALU.mult).then_inc(s.step, 1)
                v.wait_ge(s.step, base + 5 * i + 2)
                nc.vector.tensor_scalar(bitf, bitf, 0.5, None, ALU.mult).then_inc(s.step, 1)
                nc.vector.tensor_tensor(have, have, got, ALU.bitwise_or).then_inc(s.step, 1)
                v.wait_ge(s.step, base + 5 * i + 4)
                nc.vector.tensor_tensor(cand, have, nxt, ALU.bitwise_or).then_inc(s.step, 1)
            n[0] = base + 5 * 31
            v.wait_ge(s.step, n[0])
            link(nc.vector.tensor_scalar(kth, have.bitcast(F32), sgn, None, ALU.mult))
            nc.vector.scalar_tensor_tensor(out=lg[:], in0=lg[:], scalar=kth, in1=lg[:], op0=ALU.is_ge, op1=ALU.mult)\
              .then_inc(s.gate, 1)
            v.wait_ge(s.gate, 1)

        def dve_ffn(v, s):
            def split(i, e):
                hi, lo = ((hh, hl), (hh2, hl2))[e % 2]
                if e < 2:
                    v.wait_ge(s.mm2, ONE + EXPERTS * i)
                else:
                    v.wait_ge(s.mm2, ONE + EXPERTS * i + e - 1)
                for c in range(HC):
                    n = EXPERTS * HC * i + HC * e + c
                    v.wait_ge(s.high, n + 1)
                    w = slice(c * 512, c * 512 + 512)
                    nc.vector.tensor_tensor(lo[:, w], h32[:, w], hi[:, w], ALU.subtract).then_inc(s.low, 1)

            def gated(i, e):
                v.wait_ge(s.mm2, ONE + EXPERTS * i + e + 1)
                if e:
                    v.wait_ge(s.gated, ONE + EXPERTS * i + e)
                else:
                    v.wait_ge(s.b2_used, ONE + i + 1)
                for t in range(4):
                    xc = xs[:, bass.ds(i * 512 + t * P, P)]
                    m = nc.vector.scalar_tensor_tensor(out=xc, in0=ps[:, 4 + e % 2, t * P:t * P + P],
                                                       scalar=gst[:, t * EXPERTS + e:t * EXPERTS + e + 1], in1=xc,
                                                       op0=ALU.mult, op1=ALU.add)
                m.then_inc(s.gated, 1)

            with v.Fori(0, BLOCKS) as i:
                v.wait_ge(s.gated, ONE + EXPERTS * i)
                nc.vector.tensor_copy(gst, lg[:, bass.ds(i * 32, 32)]).then_inc(s.gst, 1)
                v.wait_ge(s.gst, i + 1)
                split(i, 0)
                v.wait_ge(s.gT, i + 1)
                nc.vector.tensor_copy(gtt, ps[0:EXPERTS, 6, :]).then_inc(s.gTs, 1)
                v.wait_ge(s.b2, i + 1)
                xc = xs[:, bass.ds(i * 512, 512)]
                nc.vector.tensor_tensor(xc, xc, ps[:, 7, :], ALU.add).then_inc(s.b2_used, 1)
                for e in range(1, EXPERTS):
                    split(i, e)
                    gated(i, e - 1)
                gated(i, EXPERTS - 1)

        @block.vector
        def _(v):
            dve_setup(v)
            v.wait_ge(su.x, 64)
            dve_ln(v, LN[0], False)
            dve_attn(v, 0)
            v.wait_ge(AT[0].x_new, TILES)
            dve_ln(v, LN[1], True)
            v.wait_ge(LN[1].logit_out, ONE + 8)
            dve_threshold(v, TH[0])
            dve_ffn(v, FF[0])
            v.wait_ge(FF[0].gated, ONE + BLOCKS * EXPERTS)
            dve_ln(v, LN[2], False)
            dve_attn(v, 1)
            v.wait_ge(AT[1].x_new, TILES)
            dve_ln(v, LN[3], True)
            v.wait_ge(LN[3].logit_out, ONE + 8)
            dve_threshold(v, TH[1])
            dve_ffn(v, FF[1])

        @block.gpsimd
        def _(pool):
            nc.gpsimd.memset(zero32[:], 0.0).then_inc(su.ready, 1)
            nc.gpsimd.memset(zero16[:], 0.0).then_inc(su.ready, 1)
            for a in range(2):
                s = AT[a]
                if a:
                    pool.wait_ge(FF[0].mm2, ONE + BLOCKS * EXPERTS)
                nc.gpsimd.memset(share[:], 0.0).then_inc(su.ready, 1)
                pool.wait_ge(LN[2 * a].normed, 8)
                for n in range(4):
                    xc = xs[:, 1024 * n:1024 * n + 1024].rearrange("p (t c) -> p t c", c=P)
                    nc.gpsimd.tensor_tensor(xc, xc, bp[a][:].unsqueeze(1).broadcast_to([P, 8, P]), ALU.add)\
                      .then_inc(s.bias, 1)
                pool.wait_ge(su.ready, 3 + a)

                def blocks(p, par):
                    since(pool, s.s2, 16 * (p - 1))
                    pool.wait_ge(s.split, 8 * p + SLOTS)
                    for qh in range(2):
                        for g in range(G):
                            rows = slice(32 * g, 32 * g + 32)
                            o = qh * QCOLS + g * QCOLS // G
                            for b in range(NB):
                                src = qs[rows, :].rearrange("p (s b h q) -> p s b h q", s=SLOTS, b=NB, h=2)[:, :, b, qh, :]
                                dst = qm[par][rows, o + b * SLOTS * QH:o + (b + 1) * SLOTS * QH].rearrange(
                                    "p (s q) -> p s q", s=SLOTS)
                                m = nc.gpsimd.tensor_tensor(
                                    dst, src, zero16[rows, :].unsqueeze(2).broadcast_to([32, SLOTS, QH]), ALU.add)
                            m.then_inc(s.qm, 1)

                blocks(0, 0)
                blocks(1, 1)
                with pool.Fori(1, PAIRS // 2) as i:
                    blocks(2 * i, 0)
                    blocks(2 * i + 1, 1)
                pool.wait_ge(FF[a].w_high, 2)
                nc.gpsimd.tensor_tensor(w1l, raw1, w1h, ALU.subtract).then_inc(FF[a].w_low, 1)
                nc.gpsimd.tensor_tensor(w2l, raw2, w2h, ALU.subtract).then_inc(FF[a].w_low, 1)
                f = FF[a]
                with pool.Fori(0, BLOCKS) as i:
                    for e in range(EXPERTS):
                        hi = (hh, hh2)[e % 2]
                        if e < 2:
                            pool.wait_ge(f.mm2, ONE + EXPERTS * i)
                        else:
                            pool.wait_ge(f.mm2, ONE + EXPERTS * i + e - 1)
                        for c in range(HC):
                            w = slice(c * 512, c * 512 + 512)
                            pool.wait_ge(f.gelu, ONE + EXPERTS * HC * i + HC * e + c + 1)
                            nc.gpsimd.tensor_tensor(hi[:, w], h32[:, w], zero32[:].broadcast_to([P, 512]), ALU.add)\
                              .then_inc(f.high, 1)


def kernel(**inputs):
    import numpy as np
    import concourse.bacc as bacc
    from concourse.bass_utils import run_bass_kernel_spmd as run

    g = {k: np.asarray(v) for k, v in inputs.items()}

    def heads_rows(w):
        n = w.shape[1]
        r = w.reshape(SLOTS, G, DH, n)
        z = np.zeros((SLOTS, G, DH, n), w.dtype)
        return np.concatenate([r, r, r, z], axis=2).reshape(SLOTS, P, n).transpose(1, 0, 2)

    def weights(pre, last):
        q, k, v, p = (g[f"{pre}_W{n}"] for n in ("q", "k", "v", last))
        blocks = [heads_rows(q), heads_rows(k), v[:, None, :], p[:, None, :]]
        return np.ascontiguousarray(np.concatenate(blocks, axis=1).reshape(P, BLK * P))

    def qk_bias(pre):
        q = heads_rows(g[f"{pre}_bq"][:, None])[:, :, 0]
        k = heads_rows(g[f"{pre}_bk"][:, None])[:, :, 0].copy()
        k[MROW::32, :] = MSCALE
        return np.ascontiguousarray(np.concatenate([q, k], axis=1))

    row = np.arange(P) % 32
    masks = np.stack([-((row >= 16) & (row < 24)).astype(np.float32), -((row >= 8) & (row < 16)).astype(np.float32)], 1)
    rel = g["L0_attn_b_rel_emb"]
    rel = rel[np.clip(np.arange(REL) - (T - 1), -REL_MAX, REL_MAX) + REL_MAX].T
    rel = np.tile(np.concatenate([rel, rel, rel, np.zeros_like(rel)], axis=0), (G, 1))
    arrays = {
        "x": g["L0_attn_a_x"].reshape(TILES, P, D).transpose(1, 0, 2).reshape(P, NT),
        "wa": weights("L0_attn_a", "p"), "wb": weights("L0_attn_b", "o"),
        "bias_a": qk_bias("L0_attn_a"), "bias_b": qk_bias("L0_attn_b"),
        "bv_a": np.tile(g["L0_attn_a_bv"][None, :], (P, 1)), "bv_b": np.tile(g["L0_attn_b_bv"][None, :], (P, 1)),
        "bp_a": np.tile(g["L0_attn_a_bp"][None, :], (P, 1)), "bp_b": np.tile(g["L0_attn_b_bo"][None, :], (P, 1)),
        "rel": rel, "masks": masks, "ident": np.eye(P, dtype=np.float32),
        "gate": g["L0_ffn_gate_weight"].T,
        "w1": g["L0_ffn_w1"].reshape(EXPERTS * HID, D).T,
        "b1": g["L0_ffn_b1"].reshape(EXPERTS * HC, P).T,
        "w2": g["L0_ffn_w2"].transpose(2, 0, 1).reshape(HC, P, EXPERTS, D).transpose(1, 2, 0, 3).reshape(P, EXPERTS * HID),
        "b2": g["L0_ffn_b2"],
    }
    nc = bacc.Bacc("TRN2", target_bir_lowering=False, num_devices=1)
    args = []
    for name in list(arrays):
        arrays[name] = np.ascontiguousarray(arrays[name])
        args.append(nc.dram_tensor(name, arrays[name].shape, F32, kind="ExternalInput").ap())
    args.append(nc.dram_tensor("out", (P, NT), F32, kind="ExternalOutput").ap())
    network(nc, *args)
    r = run(nc, [arrays], core_ids=[0])
    y = r.results[0]["out"]
    return np.ascontiguousarray(y.reshape(P, TILES, D).transpose(1, 0, 2).reshape(B, T, D))
```

```python
from contextlib import ExitStack

import concourse.bass as bass
from concourse import mybir

F32 = mybir.dt.float32
F16 = mybir.dt.float16
I32 = mybir.dt.int32
ALU = mybir.AluOpType
ACT = mybir.ActivationFunctionType
AX = mybir.AxisListType

P = 128
B, T, D = 16, 256, 128
NT = B * T
TILES = NT // P
HEADS, DH = 16, 8
G = 4
SLOTS = HEADS // G
KH = T // P
NB = 2
PAIRS = B // NB
GT = NB * T
QH = T // 2
QCOLS = NB * HEADS * QH
EXPERTS, HID = 8, 512
HC = HID // P
BLOCKS = NT // 512
GATED = 4 * 128 * 6
EPS = 1e-5
REL = 2 * T - 1
REL_MAX = 128
MROW = 24
MSCALE = 256.0
SCALE = float(DH) ** -0.5
ONE = 2
BLK = 10


class Setup:

    def __init__(self, sem):
        self.x = sem("x")
        self.consts = sem("consts")
        self.weights = sem("weights")
        self.alpha = sem("alpha")
        self.sign = sem("sign")
        self.binar = sem("binar")
        self.tr = sem("tr")
        self.high = sem("high")
        self.evac = sem("evac")
        self.split = sem("split")
        self.ready = sem("ready")
        self.ones = sem("ones")


class LayerNorm:

    def __init__(self, sem):
        self.stats = sem("stats")
        self.col = sem("col")
        self.sqrt = sem("sqrt")
        self.rstd = sem("rstd")
        self.cols = sem("cols")
        self.normed = sem("normed")
        self.normed2 = sem("normed2")
        self.tr = sem("tr")
        self.high = sem("high")
        self.low = sem("low")
        self.logit = sem("logit")
        self.logit_out = sem("logit_out")


class Attention:

    def __init__(self, sem):
        self.bias = sem("bias")
        self.proj = sem("proj")
        self.evac = sem("evac")
        self.t16 = sem("t16")
        self.split = sem("split")
        self.qm = sem("qm")
        self.v = sem("v")
        self.v_out = sem("v_out")
        self.e = sem("e")
        self.e_high = sem("e_high")
        self.e_low = sem("e_low")
        self.s1 = sem("s1")
        self.s1_used = sem("s1_used")
        self.r2 = sem("r2")
        self.rt = sem("rt")
        self.m3 = sem("m3")
        self.m3h = sem("m3h")
        self.m_row = sem("m_row")
        self.s2 = sem("s2")
        self.exp = sem("exp")
        self.pv = sem("pv")
        self.o_copy = sem("o_copy")
        self.ot = sem("ot")
        self.rden = sem("rden")
        self.a = sem("a")
        self.at = sem("at")
        self.at_copy = sem("at_copy")
        self.pp = sem("pp")
        self.x_new = sem("x_new")


class Threshold:

    def __init__(self, sem):
        self.cnt = sem("cnt")
        self.tot = sem("tot")
        self.step = sem("step")
        self.gate = sem("gate")


class Experts:

    def __init__(self, sem):
        self.raw = sem("raw")
        self.w_high = sem("w_high")
        self.w_low = sem("w_low")
        self.gst = sem("gst")
        self.gT = sem("gT")
        self.gTs = sem("gTs")
        self.b2 = sem("b2")
        self.b2_used = sem("b2_used")
        self.mm1 = sem("mm1")
        self.gelu = sem("gelu")
        self.high = sem("high")
        self.low = sem("low")
        self.mm2 = sem("mm2")
        self.gated = sem("gated")
        self.begun = [self.gelu, self.gated, self.b2_used, self.mm2, self.low]


def network(nc, x, wa, wb, bias_a, bias_b, bv_a, bv_b, bp_a, bp_b, rel, masks, ident, gate, w1, b1, w2, b2, out):
    with ExitStack() as ctx:
        def sb(name, shape, dt):
            return ctx.enter_context(nc.sbuf_tensor(name, shape, dt))

        xs = sb("xs", [P, NT], F32)
        xh = sb("xh", [P, NT], F16)
        xl = sb("xl", [P, NT], F16)
        stats = sb("stats", [P, TILES, 6], F32)
        lnv = sb("lnv", [P, 8, TILES], F32)
        ident32 = sb("ident32", [P, P], F32)
        ident16 = sb("ident16", [P, P], F16)
        ones16 = sb("ones16", [P, P], F16)
        mask = sb("mask", [P, 2], F32)
        wth = [sb(f"wth{n}", [P, 9 * P], F16) for n in "ab"]
        wtl = [sb(f"wtl{n}", [P, 9 * P], F16) for n in "ab"]
        wpt = [sb(f"wpt{n}", [P, P], F32) for n in "ab"]
        qkb = [sb(f"qkb{n}", [P, 2 * SLOTS], F32) for n in "ab"]
        bv = [sb(f"bv{n}", [P, P], F32) for n in "ab"]
        bp = [sb(f"bp{n}", [P, P], F32) for n in "ab"]
        zero32 = sb("zero32", [P, 1], F32)
        zero16 = sb("zero16", [P, 1], F16)
        alpha = sb("alpha", [P, BLK], F32)
        relh = sb("relh", [P, REL], F16)
        gth = sb("gth", [P, EXPERTS], F16)
        gtl = sb("gtl", [P, EXPERTS], F16)
        gt32 = sb("gt32", [P, EXPERTS], F32)
        b1s = sb("b1s", [P, EXPERTS * HC], F32)
        b2s = sb("b2s", [EXPERTS, D], F32)
        share = sb("share", [P, 16384], F16)
        w1h, w1l, w2h, w2l = (share[:, 4096 * n:4096 * n + 4096] for n in range(4))
        qm = [share[:, 8192 * n:8192 * n + 8192] for n in range(2)]
        ks = [sb(f"ks{n}", [P, SLOTS * GT], F16) for n in range(2)]
        qs = sb("qs", [P, SLOTS * GT], F16)
        x32 = sb("x32", [P, 4, 512], F32)
        t16 = sb("t16", [P, 4, 512], F16)
        vp = [sb(f"vp{n}", [P, NB * KH * HEADS * 32], F32) for n in range(2)]
        pt = sb("pt", [P, 4, KH * G * QH], F32)
        rmax = sb("rmax", [P, KH, P], F32)
        r2 = sb("r2", [P, P], F32)
        m3 = sb("m3", [P, 32], F32)
        m3h = sb("m3h", [P, 32], F16)
        osb = sb("osb", [P, SLOTS * QH], F32)
        rden = sb("rden", [P, HEADS], F32)
        asb = sb("asb", [P, P], F32)
        ats = sb("ats", [P, P], F32)
        lg = sb("lg", [P, TILES * EXPERTS], F32)
        cnt = sb("cnt", [P, 3], F16)
        tv = sb("tv", [P, 8], F32)
        ti = sb("ti", [P, 11], I32)
        flags = sb("flags", [P, 3], F32)
        big = sb("big", [P, 32768], F16)

        raw1 = big[:, 0:8192].bitcast(F32)
        raw2 = big[:, 8192:16384].bitcast(F32)
        rawa = big[:, 16384:16384 + 2 * BLK * P].bitcast(F32)
        rawb = big[:, 20480:20480 + 2 * BLK * P].bitcast(F32)
        sg = big[:, 27648:27648 + 2 * BLK * P].bitcast(F32)
        rawr = big[:, 24576:24576 + 2 * REL].bitcast(F32)
        tmp16 = big[:, 26624:26624 + 512]
        eh = [big[:, 8192 * n:8192 * n + 8192] for n in range(2)]
        el = [big[:, 16384 + 8192 * n:16384 + 8192 * n + 8192] for n in range(2)]
        h32 = big[:, 0:4096].bitcast(F32)
        hh = big[:, 4096:8192]
        hl = big[:, 8192:12288]
        hh2 = big[:, 12288:16384]
        hl2 = big[:, 16384:20480]
        gst = big[:, 20480:20544].bitcast(F32)
        gtt = big[0:EXPERTS, 20544:21568].bitcast(F32)
        zt = big[:, 31232:31744].bitcast(F32)
        junk = [big[:, 31744 + 256 * n:32000 + 256 * n] for n in range(3)]

        xn = [m.bitcast(F32).rearrange("p (a b) -> p a b", a=2) for m in (big[:, 28672:30720], qs[:])]

        ps = ctx.enter_context(nc.psum_tensor("ps", [P, 8, 512], F32))

        def region(u):
            return ps[:, 2 + u % 3, :]

        def sem(phase):
            return lambda name: ctx.enter_context(nc.semaphore(f"{phase}_{name}"))

        su = Setup(sem("setup"))
        LN = [LayerNorm(sem(f"ln{n}")) for n in range(4)]
        AT = [Attention(sem(f"attn{n}")) for n in "ab"]
        TH = [Threshold(sem(f"thr{n}")) for n in range(2)]
        FF = [Experts(sem(f"ffn{n}")) for n in range(2)]
        out_done = ctx.enter_context(nc.semaphore("out_done"))

        block = ctx.enter_context(nc.Block())

        def heads(cols, b, slot):
            return cols.rearrange("p (g b s q) -> p g b s q", g=G, b=NB, s=SLOTS)[:, :, b, slot, :]

        def since(eng, sem, n):
            if not isinstance(n, int) or n > 0:
                eng.wait_ge(sem, n)

        @block.sync
        def _(sp):
            for n in range(4):
                sp.dma_start(xs[:, 1024 * n:1024 * n + 1024], x[:, 1024 * n:1024 * n + 1024]).then_inc(su.x, 16)
            for dst, src in ((ident32, ident), (mask, masks), (qkb[0], bias_a), (qkb[1], bias_b), (bv[0], bv_a),
                             (bv[1], bv_b), (bp[0], bp_a), (bp[1], bp_b), (gt32, gate), (b1s, b1), (b2s, b2)):
                sp.dma_start(dst[:], src).then_inc(su.consts, 16)
            for dst, src in ((rawa, wa), (rawb, wb), (rawr, rel)):
                sp.dma_start(dst, src).then_inc(su.weights, 16)
            for s in FF:
                for sem in s.begun:
                    sp.sem_inc(sem, ONE)
            for a in range(2):
                s = AT[a]
                if a == 0:
                    for dst, src in ((raw1, w1), (raw2, w2)):
                        sp.dma_start(dst, src).then_inc(FF[0].raw, 16)
                with sp.Fori(0, PAIRS // 2) as i:
                    for k in range(4):
                        sp.wait_ge(s.m3h, 4 * i + k + 1)
                        dst = qm[k // 2][MROW:MROW + 1, k % 2 * QCOLS:(k % 2 + 1) * QCOLS]
                        sp.dma_start(dst.rearrange("p (k q) -> p k q", q=32), m3h[:]).then_inc(s.m_row, 16)
                if a == 1:
                    sp.wait_ge(s.s2, 32 * PAIRS)
                    for dst, src in ((raw1, w1), (raw2, w2)):
                        sp.dma_start(dst, src).then_inc(FF[1].raw, 16)
            for n in range(BLOCKS):
                sp.wait_ge(FF[1].gated, ONE + EXPERTS * (n + 1))
                sp.dma_start(out[:, 512 * n:512 * n + 512], xs[:, 512 * n:512 * n + 512]).then_inc(out_done, 16)
            sp.wait_ge(out_done, 16 * BLOCKS)

        QUERIES = range(4)
        KEYS_VALUES = range(4, 10)

        def beside(p, qh, projections, rel_on):
            t, pn = 2 * p + qh + 1, p + 1 + qh
            return [("relative", k, t) for k in range(16)] * rel_on + [("first", k, t) for k in range(16)] \
                + [("project", k, pn) for k in projections[:2]] + [("maxima", 0, t)] \
                + [("project", k, pn) for k in projections[2:]]

        def before(rel_on):
            return [("project", k, 0) for k in range(10)] + beside(0, -1, [], rel_on) + [("project", k, 1) for k in QUERIES]

        def portion(v, part, items, projections):
            early, late = len(projections[:2]), len(projections[2:])
            n = len(items) - early - late - 1
            if v < 6:
                c = 2 * v + part
                return range(n * c // 12, n * (c + 1) // 12 + (early + 1 if c == 11 else 0))
            n += early + 1
            return range(n + late * (v - 6) // 2, n + late * (v - 5) // 2) if part else []

        def bank(n):
            return ps[:, (0, 1, 5)[n % 3], :]

        def opening(work, count, first, rest):
            first(0)
            first(1)
            for n in (0, 1):
                rest(n)
                first(n + 2)
            for n in range(10):
                work(n)
            for n in range(2, 8):
                rest(n)
                if n < 6:
                    first(n + 2)
            for n in range(10, count):
                work(n)

        def closing(v, first, rest, lag):
            if v >= lag and v - lag < 7:
                first(v - lag)
            if v >= lag + 2:
                rest(v - lag - 2)

        def pe_setup(pe):
            pe.wait_ge(su.consts, 176)
            pe.wait_ge(su.weights, 48)
            for k in range(2 * BLK):
                raw = rawa if k < BLK else rawb
                if k == 0:
                    pe.wait_ge(su.binar, 1)
                if k >= 4:
                    pe.wait_ge(su.evac, k - 3)
                kk = k % BLK
                nc.tensor.transpose(ps[:, k % 4, 0:P], raw[:, kk * P:kk * P + P], ident32[:]).then_inc(su.tr, 1)

        def pe_ln(pe, s, after):
            banks = (0, 1) if after else (6, 7)

            def transposes(n):
                j = n % 2
                pe.wait_ge(s.normed, n + 1)
                pe.wait_ge(s.normed2, n + 1)
                since(pe, s.low, n - 1)
                for t in range(4):
                    m = nc.tensor.transpose(ps[:, banks[j], t * P:t * P + P], xn[after][:, j, t * P:t * P + P],
                                            ident32[:])
                m.then_inc(s.tr, 1)

            def logits(n):
                if not after:
                    return
                pe.wait_ge(s.low, n + 1)
                for t in range(4):
                    k = n * 4 + t
                    o = ps[:, 5, k * EXPERTS:(k + 1) * EXPERTS]
                    nc.tensor.matmul(o, xh[:, k * P:k * P + P], gth[:], start=True, stop=False)
                    nc.tensor.matmul(o, xh[:, k * P:k * P + P], gtl[:], start=False, stop=False)
                    m = nc.tensor.matmul(o, xl[:, k * P:k * P + P], gth[:], start=False, stop=True)
                m.then_inc(s.logit, 1)

            return transposes, logits

        def pe_attn(pe, a):
            s = AT[a]
            rel_on = a == 1

            def left(kind, k, x):
                if kind == "relative":
                    pe.wait_ge(s.e_low, 16 * x + k + 1)
                elif kind == "first":
                    pe.wait_ge(s.s1_used, 16 * x + k + 1)
                elif kind == "maxima":
                    pe.wait_ge(s.m3, x + 1)
                elif k < 8:
                    pe.wait_ge(s.evac, 8 * x + k + 1)
                else:
                    pe.wait_ge(s.v_out, 4 * x + 2 * (k - 7))

            def prep(o, k, p):
                if k < 8:
                    tok = bass.ds(p * GT, GT)
                    w = slice(k * P, k * P + P)
                    nc.tensor.matmul(o, wth[a][:, w], xh[:, tok], start=True, stop=False)
                    nc.tensor.matmul(o, wth[a][:, w], xl[:, tok], start=False, stop=False)
                    nc.tensor.matmul(o, wtl[a][:, w], xh[:, tok], start=False, stop=True).then_inc(s.proj, 1)
                else:
                    for j in range(2):
                        tok = bass.ds(p * GT + (2 * (k - 8) + j) * P, P)
                        oj = o[:, j * P:j * P + P]
                        w = slice(8 * P, 9 * P)
                        nc.tensor.matmul(oj, xh[:, tok], wth[a][:, w], start=True, stop=False)
                        nc.tensor.matmul(oj, xh[:, tok], wtl[a][:, w], start=False, stop=False)
                        m = nc.tensor.matmul(oj, xl[:, tok], wth[a][:, w], start=False, stop=True)
                    m.then_inc(s.v, 1)

            def relative(o, u, p, par, qh):
                kh, qc = u // 8, u % 8
                if u == 0:
                    pe.wait_ge(s.qm, 8 * p + 4 * qh + 4)
                cols = qm[par][:, qh * QCOLS:(qh + 1) * QCOLS]
                for j in range(16):
                    q = qc * 16 + j
                    w0 = T - 1 - (qh * QH + q) + kh * P
                    m = nc.tensor.matmul(o[:, j * 32:j * 32 + 32], relh[:, w0:w0 + P],
                                         cols[:, q:q + (NB * HEADS - 1) * QH + 1:QH], start=True, stop=True)
                m.then_inc(s.e, 1)

            def scores(o, b, slot, kh, par, qh, low):
                o = o.rearrange("p (g q) -> p g q", g=G)
                kcol = slot * GT + b * T + kh * P
                m = nc.tensor.matmul(o, ks[par][:, kcol:kcol + P],
                                     heads(qm[par][:, qh * QCOLS:(qh + 1) * QCOLS], b, slot), start=True, stop=not rel_on)
                if rel_on:
                    e = slice(kh * QCOLS, (kh + 1) * QCOLS)
                    m = nc.tensor.matmul(o, ident16[:], heads(eh[qh][:, e], b, slot), start=False, stop=not low)
                    if low:
                        m = nc.tensor.matmul(o, ident16[:], heads(el[qh][:, e], b, slot), start=False, stop=True)
                return m

            def first_pass(o, w, p, par, qh):
                b, slot, kh = w // 8, w // 2 % 4, w % 2
                if w == 0:
                    pe.wait_ge(s.split, 8 * (p + 1))
                    pe.wait_ge(s.qm, 8 * p + 4 * qh + 4)
                    if rel_on:
                        pe.wait_ge(s.e_high, 16 * (2 * p + qh + 1))
                scores(o, b, slot, kh, par, qh, False).then_inc(s.s1, 1)

            def max_transpose(o, t):
                pe.wait_ge(s.r2, t + 1)
                nc.tensor.transpose(o[:, 0:P], r2[:], ident32[:]).then_inc(s.rt, 1)

            def work(items, n, p, par, qh):
                if n >= 3:
                    left(*items[n - 3])
                kind, k, x = items[n]
                if kind == "project":
                    prep(bank(n), k, x)
                elif kind == "relative":
                    relative(bank(n), k, p, par, qh)
                elif kind == "first":
                    first_pass(bank(n), k, p, par, qh)
                else:
                    max_transpose(bank(n), x)

            def second_pass(v, t, par, qh):
                b, slot = v // 4, v % 4
                if v == 0:
                    pe.wait_ge(s.m_row, 16 * (t + 1))
                    if rel_on:
                        pe.wait_ge(s.e_low, 16 * (t + 1))
                for kh in range(KH):
                    u = KH * v + kh
                    if u == 0:
                        since(pe, s.exp, 16 * t)
                    elif u >= 3:
                        pe.wait_ge(s.exp, 16 * t + u - 2)
                    scores(region(u), b, slot, kh, par, qh, True).then_inc(s.s2, 1)

            def pv(v, t, p, par):
                b, slot = v // 4, v % 4
                pe.wait_ge(s.exp, 16 * t + 2 * v + 2)
                if slot == 0:
                    since(pe, s.o_copy, 2 * t + b)
                    pe.wait_ge(s.v_out, 4 * (p + 1))
                for kh in range(KH):
                    for g in range(G):
                        v0 = ((b * KH + kh) * HEADS + slot * G + g) * 32
                        m = nc.tensor.matmul(ps[32 * g:32 * g + 32, 6, slot * QH:slot * QH + QH], vp[par][:, v0:v0 + 32],
                                             pt[:, v % 4, (kh * G + g) * QH:(kh * G + g + 1) * QH], start=kh == 0,
                                             stop=kh == KH - 1, tile_position=(0, 32 * g))
                m.then_inc(s.pv, 1)

            def out_transpose(n):
                pe.wait_ge(s.o_copy, n + 1)
                since(pe, s.x_new, n)
                for slot in range(SLOTS):
                    m = nc.tensor.transpose(ps[:, 7, slot * QH:slot * QH + QH], osb[:, slot * QH:slot * QH + QH],
                                            ident32[:])
                m.then_inc(s.ot, 1)

            def back_transpose(n):
                pe.wait_ge(s.a, n + 1)
                nc.tensor.transpose(ps[:, 7, 0:P], asb[:], ident32[:]).then_inc(s.at, 1)

            def project(n):
                pe.wait_ge(s.at_copy, n + 1)
                nc.tensor.matmul(ps[:, 7, 0:P], ats[:], wpt[a][:], start=True, stop=True).then_inc(s.pp, 1)

            def step(p, par, qh, projections, first=False, last=False):
                t = 2 * p + qh
                pn, parn, qn = (p, par, 1) if qh == 0 else (p + 1, 1 - par, 0)
                items = beside(p, qh, projections, rel_on)
                for v in range(8):
                    second_pass(v, t, par, qh)
                    if v == 0 and not last:
                        if qh == 0:
                            pe.wait_ge(s.evac, 8 * PAIRS if isinstance(p, int) and p == PAIRS - 1 else 8 * p + 12)
                        else:
                            pe.wait_ge(s.v_out, 4 * (p + 2))
                    for part in range(2):
                        if part == 0 and not first:
                            if v == 0:
                                pv(7, t - 1, p if qh else p - 1, par if qh else 1 - par)
                            if v == 1:
                                out_transpose(2 * t - 1)
                            if v == 2:
                                back_transpose(2 * t - 1)
                            if v == 3:
                                project(2 * t - 1)
                        if part == 0 and v == 5:
                            out_transpose(2 * t)
                        if part == 1 and v:
                            pv(v - 1, t, p, par)
                        if part == 1 and v == 6:
                            back_transpose(2 * t)
                        if part == 1 and v == 7:
                            project(2 * t)
                        for n in portion(v, part, items, projections) if not last else []:
                            work(items, n, pn, parn, qn)
                    if last:
                        closing(v, *next_ln, 1)

            items = before(rel_on)

            def begin(n):
                if n == 0:
                    pe.wait_ge(LN[2 * a].low, 1)
                if items[n] == ("project", 0, 1):
                    pe.wait_ge(LN[2 * a].low, 8)
                work(items, n, 0, 0, 0)

            next_ln = pe_ln(pe, LN[2 * a + 1], 1)
            opening(begin, len(items), *pe_ln(pe, LN[2 * a], 0))
            step(0, 0, 0, KEYS_VALUES, first=True)
            with pe.Fori(0, PAIRS // 2 - 1) as i:
                for par in range(2):
                    step(2 * i + par, par, 1, QUERIES)
                    step(2 * i + par + 1, 1 - par, 0, KEYS_VALUES)
            step(PAIRS - 2, 0, 1, [])
            step(PAIRS - 1, 1, 0, [])
            step(PAIRS - 1, 1, 1, [], last=True)
            t = 2 * PAIRS - 1
            pv(7, t, PAIRS - 1, 1)
            out_transpose(2 * t + 1)
            back_transpose(2 * t + 1)
            project(2 * t + 1)
            transposes, logits = next_ln
            logits(5)
            transposes(7)
            logits(6)
            logits(7)

        def pe_threshold(pe, s):
            pe.wait_ge(s.cnt, 1)
            nc.tensor.matmul(ps[:, 6, 0:1], ones16[:], cnt[:, 0:1], start=True, stop=True).then_inc(s.tot, 1)
            with pe.Fori(0, 15) as i:
                pe.wait_ge(s.cnt, 3 * i + 4)
                nc.tensor.matmul(ps[:, 6, 0:3], ones16[:], cnt[:], start=True, stop=True).then_inc(s.tot, 1)
            pe.wait_ge(s.cnt, 47)
            nc.tensor.matmul(ps[:, 6, 0:1], ones16[:], cnt[:, 0:1], start=True, stop=True).then_inc(s.tot, 1)

        def pe_ffn(pe, s, ln):
            def up(i, e):
                for c in range(HC):
                    n = HC * (EXPERTS * i + e) + c
                    since(pe, s.gelu, ONE + n - HC + 1)
                    w = slice(e * HID + c * P, e * HID + c * P + P)
                    tok = bass.ds(i * 512, 512)
                    nc.tensor.matmul(ps[:, c, :], w1h[:, w], xh[:, tok], start=True, stop=False)
                    nc.tensor.matmul(ps[:, c, :], w1h[:, w], xl[:, tok], start=False, stop=False)
                    nc.tensor.matmul(ps[:, c, :], w1l[:, w], xh[:, tok], start=False, stop=True).then_inc(s.mm1, 1)

            def down(i, e):
                n = EXPERTS * i + e
                hi, lo = ((hh, hl), (hh2, hl2))[e % 2]
                pe.wait_ge(s.low, ONE + HC * (n + 1))
                pe.wait_ge(s.high, HC * (n + 1))
                pe.wait_ge(s.gated, ONE + n - 1)
                for t in range(4):
                    for c in range(HC):
                        h = slice(c * 512 + t * P, c * 512 + t * P + P)
                        w = slice((e * HC + c) * P, (e * HC + c + 1) * P)
                        o = ps[:, 4 + e % 2, t * P:t * P + P]
                        nc.tensor.matmul(o, hi[:, h], w2h[:, w], start=c == 0, stop=False)
                        nc.tensor.matmul(o, hi[:, h], w2l[:, w], start=False, stop=False)
                        m = nc.tensor.matmul(o, lo[:, h], w2h[:, w], start=False, stop=c == HC - 1)
                m.then_inc(s.mm2, 1)

            def tokens(i, last):
                for e in range(1, EXPERTS + 1 - last):
                    up(i + e // EXPERTS, e % EXPERTS)
                    if e == 2:
                        pe.wait_ge(s.gst, i + 1)
                        pe.wait_ge(s.b2_used, ONE + i)
                        for t in range(4):
                            m = nc.tensor.transpose(ps[0:EXPERTS, 6, t * P:t * P + P],
                                                    gst[:, t * EXPERTS:(t + 1) * EXPERTS], ident32[:])
                        m.then_inc(s.gT, 1)
                    if e == 3:
                        pe.wait_ge(s.gTs, i + 1)
                        for t in range(4):
                            m = nc.tensor.matmul(ps[:, 7, t * P:t * P + P], gtt[:, t * P:t * P + P], b2s[:],
                                                 start=True, stop=True)
                        m.then_inc(s.b2, 1)
                    down(i, e - 1)

            pe.wait_ge(ln.low, 8)
            pe.wait_ge(ln.logit_out, 1)
            pe.wait_ge(s.w_high, 2)
            pe.wait_ge(s.w_low, 2)
            up(0, 0)
            with pe.Fori(0, BLOCKS - 1) as i:
                tokens(i, False)
            tokens(BLOCKS - 1, True)
            down(BLOCKS - 1, EXPERTS - 1)

        @block.tensor
        def _(pe):
            pe_setup(pe)
            pe.wait_ge(su.evac, 2 * BLK)
            pe.wait_ge(su.split, 1)
            pe_attn(pe, 0)
            pe_threshold(pe, TH[0])
            pe_ffn(pe, FF[0], LN[1])
            pe_attn(pe, 1)
            pe_threshold(pe, TH[1])
            pe_ffn(pe, FF[1], LN[3])

        def act_columns(act, s, k, tiles):
            act.wait_ge(s.col, k + 1)
            nc.scalar.activation(lnv[:, 3, tiles], lnv[:, 2, tiles], ACT.Sqrt).then_inc(s.sqrt, 1)
            act.wait_ge(s.cols, k + 1)

        def act_ln(act, s, after):
            banks = (0, 1) if after else (6, 7)

            def normalise(n):
                since(act, s.tr, n - 1)
                for t in range(2, 4):
                    k = n * 4 + t
                    m = nc.scalar.activation(xn[after][:, n % 2, t * P:t * P + P], xs[:, k * P:k * P + P], ACT.Identity,
                                             bias=lnv[:, 3, k:k + 1], scale=lnv[:, 7, k:k + 1])
                m.then_inc(s.normed2, 1)

            def high(n):
                act.wait_ge(s.tr, n + 1)
                nc.scalar.activation(xh[:, n * 512:n * 512 + 512], ps[:, banks[n % 2], :], ACT.Copy).then_inc(s.high, 1)

            return normalise, high

        def act_attn(act, a):
            s = AT[a]
            rel_on = a == 1

            def evacuate(o, k, p):
                act.wait_ge(s.proj, 8 * p + k + 1)
                since(act, s.split, 8 * p + k - 3)
                nc.scalar.activation(x32[:, k % 4, :], o, ACT.Identity, bias=qkb[a][:, k:k + 1])\
                  .then_inc(s.evac, 1)

            def relative_high(o, u, t, qh):
                kh, qc = u // 8, u % 8
                act.wait_ge(s.e, 16 * t + u + 1)
                if u == 0:
                    since(act, s.s2, 16 * (t - 1))
                src = o.rearrange("p (q n) -> p n q", q=16)
                dst = eh[qh][:, kh * QCOLS:(kh + 1) * QCOLS].rearrange("p (n q) -> p n q", q=QH)[
                    :, :, qc * 16:qc * 16 + 16]
                nc.scalar.activation(dst, src, ACT.Copy).then_inc(s.e_high, 1)

            def work(items, n, qh):
                kind, k, x = items[n]
                if kind == "project" and k < 8:
                    evacuate(bank(n), k, x)
                elif kind == "relative":
                    relative_high(bank(n), k, x, qh)

            def exponential(v, t):
                since(act, s.pv, 8 * t + v - 3)
                for kh in range(KH):
                    u = KH * v + kh
                    act.wait_ge(s.s2, 16 * t + u + 1)
                    nc.scalar.activation(pt[:, v % 4, 512 * kh:512 * kh + 512], region(u), ACT.Exp, scale=SCALE)\
                       .then_inc(s.exp, 1)

            def out_copy(n):
                act.wait_ge(s.pv, 4 * (n + 1))
                since(act, s.ot, n)
                nc.scalar.activation(osb[:], ps[:, 6, :], ACT.Copy).then_inc(s.o_copy, 1)

            def back_copy(n):
                act.wait_ge(s.at, n + 1)
                nc.scalar.activation(ats[:], ps[:, 7, 0:P], ACT.Copy).then_inc(s.at_copy, 1)

            def step(p, par, qh, projections, first=False, last=False):
                t = 2 * p + qh
                items = beside(p, qh, projections, rel_on)
                for v in range(8):
                    exponential(v, t)
                    if not first:
                        if v == 0:
                            out_copy(2 * t - 1)
                        if v == 2:
                            back_copy(2 * t - 1)
                    for part in range(2):
                        if part == 1 and v == 4:
                            out_copy(2 * t)
                        if part == 1 and v == 6:
                            back_copy(2 * t)
                        for n in portion(v, part, items, projections) if not last else []:
                            work(items, n, 1 - qh)
                    if last:
                        if v == 0:
                            act_columns(act, LN[2 * a + 1], 0, slice(0, TILES - 4))
                        closing(v, *next_ln, 0)

            items = before(rel_on)
            next_ln = act_ln(act, LN[2 * a + 1], 1)
            if a:
                act_columns(act, LN[2], 0, slice(0, TILES))
            opening(lambda n: work(items, n, 0), len(items), *act_ln(act, LN[2 * a], 0))
            step(0, 0, 0, KEYS_VALUES, first=True)
            with act.Fori(0, PAIRS // 2 - 1) as i:
                for par in range(2):
                    step(2 * i + par, par, 1, QUERIES)
                    step(2 * i + par + 1, 1 - par, 0, KEYS_VALUES)
            step(PAIRS - 2, 0, 1, [])
            step(PAIRS - 1, 1, 0, [])
            step(PAIRS - 1, 1, 1, [], last=True)
            out_copy(4 * PAIRS - 1)
            back_copy(4 * PAIRS - 1)
            next_ln[1](6)
            act_columns(act, LN[2 * a + 1], 1, slice(TILES - 4, TILES))
            for stage in next_ln:
                stage(7)

        def act_ffn(act, s):
            def gelu(i, e):
                for c in range(HC):
                    n = HC * (EXPERTS * i + e) + c
                    act.wait_ge(s.mm1, n + 1)
                    since(act, s.low, ONE + n - HC + 1)
                    nc.scalar.activation(h32[:, c * 512:c * 512 + 512], ps[:, c, :], ACT.Gelu_apprx_tanh,
                                         bias=b1s[:, e * HC + c:e * HC + c + 1]).then_inc(s.gelu, 1)

            gelu(0, 0)
            with act.Fori(0, BLOCKS - 1) as i:
                for e in range(1, EXPERTS + 1):
                    gelu(i + e // EXPERTS, e % EXPERTS)
            for e in range(1, EXPERTS):
                gelu(BLOCKS - 1, e)

        @block.scalar
        def _(act):
            act_columns(act, LN[0], 0, slice(0, TILES))
            act.wait_ge(su.weights, 48)
            act.wait_ge(su.ones, 5)
            nc.scalar.activation(sg, rawa, ACT.Sign).then_inc(su.sign, 1)
            for k in range(2 * BLK):
                a, kk = k // BLK, k % BLK
                if kk < 9:
                    act.wait_ge(su.tr, k + 1)
                    nc.scalar.activation(wth[a][:, kk * P:kk * P + P], ps[:, k % 4, 0:P], ACT.Copy).then_inc(su.high, 1)
            for a in range(2):
                act_attn(act, a)
                act.wait_ge(FF[a].raw, 32)
                act.wait_ge(AT[a].s2, 32 * PAIRS)
                nc.scalar.activation(w1h, raw1, ACT.Copy).then_inc(FF[a].w_high, 1)
                nc.scalar.activation(w2h, raw2, ACT.Copy).then_inc(FF[a].w_high, 1)
                act_ffn(act, FF[a])

        def dve_setup(v):
            nc.vector.memset(vp[0][:], 0.0).then_inc(su.ones, 1)
            nc.vector.memset(vp[1][:], 0.0).then_inc(su.ones, 1)
            nc.vector.memset(ones16[:], 1.0).then_inc(su.ones, 1)
            v.wait_ge(su.ones, 3)
            for n in range(2):
                nc.vector.memset(vp[n][:].rearrange("p (n c) -> p n c", c=32)[:, :, 8:9], 1.0).then_inc(su.ones, 1)
            v.wait_ge(su.x, 64)
            with v.Fori(0, 4) as i:
                for k in range(8):
                    statistics(8 * i + k, LN[0])
            dve_columns(v, LN[0], 0, slice(0, TILES))
            v.wait_ge(su.weights, 48)
            v.wait_ge(su.consts, 176)
            nc.vector.tensor_copy(ident16[:], ident32[:]).then_inc(su.alpha, 1)
            nc.vector.tensor_reduce(alpha[:], rawa.rearrange("p (n c) -> p n c", c=P), AX.X, ALU.add,
                                    apply_absolute_value=True).then_inc(su.alpha, 1)
            v.wait_ge(su.alpha, 2)
            nc.vector.tensor_scalar(alpha[:], alpha[:], 1.0 / D, None, ALU.mult).then_inc(su.alpha, 1)
            v.wait_ge(su.sign, 1)
            v.wait_ge(su.alpha, 3)
            nc.vector.tensor_tensor(sg, sg, rawa, ALU.subtract).then_inc(su.alpha, 1)
            v.wait_ge(su.alpha, 4)
            nc.vector.tensor_tensor(rawa, rawa, sg, ALU.add).then_inc(su.alpha, 1)
            v.wait_ge(su.alpha, 5)
            blocks = rawa.rearrange("p (n c) -> p n c", c=P)
            nc.vector.tensor_tensor(blocks, blocks, alpha[:].unsqueeze(2).broadcast_to([P, BLK, P]), ALU.mult)\
              .then_inc(su.binar, 1)
            for k in range(2 * BLK):
                a, kk = k // BLK, k % BLK
                v.wait_ge(su.tr, k + 1)
                src = ps[:, k % 4, 0:P]
                if kk < 9:
                    w = slice(kk * P, kk * P + P)
                    v.wait_ge(su.high, 9 * a + kk + 1)
                    nc.vector.tensor_tensor(wtl[a][:, w], src, wth[a][:, w], ALU.subtract).then_inc(su.evac, 1)
                else:
                    nc.vector.tensor_copy(wpt[a][:], src).then_inc(su.evac, 1)
            n = 5
            for hi, lo, raw in ((gth, gtl, gt32[:]),):
                nc.vector.tensor_copy(hi[:], raw).then_inc(su.alpha, 1)
                n += 1
                v.wait_ge(su.alpha, n)
                nc.vector.tensor_tensor(lo[:], raw, hi[:], ALU.subtract).then_inc(su.alpha, 1)
                n += 1
            nc.vector.tensor_copy(tmp16[:, 0:REL], rawr).then_inc(su.alpha, 1)
            n += 1
            v.wait_ge(su.alpha, n)
            nc.vector.scalar_tensor_tensor(out=relh[:], in0=tmp16[:, 0:REL], scalar=mask[:, 1:2], in1=rawr,
                                           op0=ALU.mult, op1=ALU.add).then_inc(su.split, 1)

        def statistics(k, s):
            nc.vector.bn_stats(stats[:, bass.ds(k, 1), :].rearrange("p a b -> p (a b)"), xs[:, bass.ds(k * P, P)])\
              .then_inc(s.stats, 1)

        def dve_columns(v, s, k, tiles):
            v.wait_ge(s.stats, tiles.stop)
            n = [11 * k]

            def link(m):
                n[0] += 1
                m.then_inc(s.rstd, 1)
                v.wait_ge(s.rstd, n[0])

            me, ve, mo, vo = (stats[:, tiles, j] for j in (1, 2, 4, 5))
            c = [lnv[:, j, tiles] for j in range(8)]
            link(nc.vector.tensor_tensor(c[0], me, mo, ALU.add))
            link(nc.vector.tensor_tensor(c[1], me, mo, ALU.subtract))
            link(nc.vector.tensor_tensor(c[4], ve, vo, ALU.add))
            link(nc.vector.tensor_scalar(c[0], c[0], 0.5, None, ALU.mult))
            link(nc.vector.tensor_tensor(c[1], c[1], c[1], ALU.mult))
            link(nc.vector.tensor_scalar(c[4], c[4], 1.0 / D, EPS, ALU.mult, ALU.add))
            nc.vector.scalar_tensor_tensor(out=c[2], in0=c[1], scalar=0.25, in1=c[4], op0=ALU.mult, op1=ALU.add)\
              .then_inc(s.col, 1)
            v.wait_ge(s.sqrt, k + 1)
            link(nc.vector.reciprocal(c[5], c[3]))
            v.wait_ge(s.col, k + 1)
            link(nc.vector.tensor_tensor(c[6], c[5], c[5], ALU.mult))
            link(nc.vector.tensor_tensor(c[6], c[6], c[2], ALU.mult))
            link(nc.vector.tensor_scalar(c[6], c[6], -0.5, 1.5, ALU.mult, ALU.add))
            link(nc.vector.tensor_tensor(c[7], c[6], c[5], ALU.mult))
            nc.vector.scalar_tensor_tensor(out=c[3], in0=c[0], scalar=-1.0, in1=c[7], op0=ALU.mult, op1=ALU.mult)\
              .then_inc(s.cols, 1)

        def dve_ln(v, s, after):
            banks = (0, 1) if after else (6, 7)

            def normalise(n):
                since(v, s.tr, n - 1)
                for t in range(2):
                    k = n * 4 + t
                    m = nc.vector.tensor_scalar(xn[after][:, n % 2, t * P:t * P + P], xs[:, k * P:k * P + P],
                                                lnv[:, 0, k:k + 1], lnv[:, 7, k:k + 1], ALU.subtract, ALU.mult)
                m.then_inc(s.normed, 1)

            def low(n):
                v.wait_ge(s.high, n + 1)
                nc.vector.tensor_tensor(xl[:, n * 512:n * 512 + 512], ps[:, banks[n % 2], :],
                                        xh[:, n * 512:n * 512 + 512], ALU.subtract).then_inc(s.low, 1)

            return normalise, low

        def dve_attn(v, a):
            s = AT[a]
            rel_on = a == 1

            def prep(o, k, p, par):
                if k < 8:
                    if k == 0:
                        since(v, s.qm, 8 * p)
                    if k == 4:
                        since(v, s.s2, 32 * (p - 1))
                    v.wait_ge(s.evac, 8 * p + k + 1)
                    nc.vector.tensor_copy(t16[:, k % 4, :], x32[:, k % 4, :]).then_inc(s.t16, 1)
                    v.wait_ge(s.t16, 8 * p + k + 1)
                    dst, c = (qs, 0) if k < SLOTS else (ks[par], 1)
                    nc.vector.scalar_tensor_tensor(out=dst[:, (k % SLOTS) * GT:(k % SLOTS + 1) * GT],
                                                   in0=t16[:, k % 4, :], scalar=mask[:, c:c + 1], in1=x32[:, k % 4, :],
                                                   op0=ALU.mult, op1=ALU.add).then_inc(s.split, 1)
                else:
                    v.wait_ge(s.v, 2 * p + k - 7)
                    if k == 8:
                        since(v, s.pv, 16 * (p - 1))
                    for j in range(2):
                        t = 2 * (k - 8) + j
                        nc.vector.tensor_tensor(
                            vp[par][:, t * 512:t * 512 + 512].rearrange("p (n c) -> p n c", c=32)[:, :, 0:DH],
                            o[:, j * P:j * P + P].rearrange("p (n c) -> p n c", c=DH),
                            bv[a][:].rearrange("p (n c) -> p n c", c=DH), ALU.add).then_inc(s.v_out, 1)

            def relative_low(o, u, t, qh):
                kh, qc = u // 8, u % 8
                v.wait_ge(s.e_high, 16 * t + u + 1)
                src = o.rearrange("p (q n) -> p n q", q=16)
                hi, lo = (e[qh][:, kh * QCOLS:(kh + 1) * QCOLS].rearrange("p (n q) -> p n q", q=QH)[
                    :, :, qc * 16:qc * 16 + 16] for e in (eh, el))
                nc.vector.tensor_tensor(lo, src, hi, ALU.subtract).then_inc(s.e_low, 1)

            def reduce(o, w, t):
                b, slot, kh = w // 8, w // 2 % 4, w % 2
                v.wait_ge(s.s1, 16 * t + w + 1)
                dst = rmax[:, kh, :].rearrange("p (g b s q) -> p g b s q", g=G, b=NB, s=SLOTS)[:, :, b, slot, :]
                nc.vector.tensor_reduce(dst, o.rearrange("p (g q k) -> p g q k", g=G, k=32), AX.X, ALU.max,
                                        apply_transpose=True).then_inc(s.s1_used, 1)
                if w == 15:
                    v.wait_ge(s.s1_used, 16 * (t + 1))
                    nc.vector.tensor_tensor(r2[:], rmax[:, 0, :], rmax[:, 1, :], ALU.max).then_inc(s.r2, 1)

            def maxima(o, t):
                v.wait_ge(s.rt, t + 1)
                nc.vector.tensor_reduce(m3[:], o[:, 0:P].rearrange("p (k q) -> p q k", k=4), AX.X, ALU.max)\
                  .then_inc(s.m3, 1)
                v.wait_ge(s.m3, t + 1)
                nc.vector.tensor_scalar(m3h[:], m3[:], -1.0 / MSCALE, None, ALU.mult).then_inc(s.m3h, 1)

            def work(items, n, par, qh):
                kind, k, x = items[n]
                if kind == "project":
                    prep(bank(n), k, x, par)
                elif kind == "relative":
                    relative_low(bank(n), k, x, qh)
                elif kind == "first":
                    reduce(bank(n), k, x)
                else:
                    maxima(bank(n), x)

            def normalise(n):
                v.wait_ge(s.ot, n + 1)
                o = ps[:, 7, :].rearrange("p (h c) -> p h c", c=32)
                nc.vector.reciprocal(rden[:].unsqueeze(2), o[:, :, DH:DH + 1]).then_inc(s.rden, 1)
                v.wait_ge(s.rden, n + 1)
                nc.vector.tensor_tensor(asb[:].rearrange("p (h c) -> p h c", c=DH), o[:, :, 0:DH],
                                        rden[:].unsqueeze(2).broadcast_to([P, HEADS, DH]), ALU.mult).then_inc(s.a, 1)

            def residual(n, tile):
                v.wait_ge(s.pp, n + 1)
                xc = xs[:, bass.ds(tile * P, P)]
                nc.vector.tensor_tensor(xc, xc, ps[:, 7, 0:P], ALU.add).then_inc(s.x_new, 1)

            def after(n, tile):
                v.wait_ge(s.x_new, n + 1)
                statistics(tile, LN[2 * a + 1])

            def step(p, par, qh, projections, first=False, last=False):
                t = 2 * p + qh
                items = beside(p, qh, projections, rel_on)
                for c in range(8):
                    if not first:
                        if c == 1:
                            normalise(2 * t - 1)
                        if c == 3:
                            residual(2 * t - 1, 4 * (p if qh else p - 1) + 2 + (1 - qh))
                        if c in (1, 4):
                            after(2 * t - 2 + c // 4, 4 * (p if qh else p - 1) + c // 2 + (1 - qh))
                    if c == 5:
                        normalise(2 * t)
                    for part in range(2):
                        row = list(portion(c, part, items, projections)) if not last else []
                        if projections and row and items[row[-1]][0] == "maxima":
                            row[-2:] = reversed(row[-2:])
                        for n in row:
                            work(items, n, par if qh else 1 - par, 1 - qh)
                    if last:
                        if c == 0:
                            v.wait_ge(s.qm, 8 * PAIRS)
                            dve_columns(v, LN[2 * a + 1], 0, slice(0, TILES - 4))
                        closing(c, *next_ln, 0)
                    if c == 7:
                        residual(2 * t, 4 * p + qh)

            items = before(rel_on)
            next_ln = dve_ln(v, LN[2 * a + 1], 1)
            if a:
                dve_columns(v, LN[2], 0, slice(0, TILES))
            opening(lambda n: work(items, n, items[n][2], 0), len(items), *dve_ln(v, LN[2 * a], 0))
            v.wait_ge(s.bias, 4)
            step(0, 0, 0, KEYS_VALUES, first=True)
            with v.Fori(0, PAIRS // 2 - 1) as i:
                for par in range(2):
                    step(2 * i + par, par, 1, QUERIES)
                    step(2 * i + par + 1, 1 - par, 0, KEYS_VALUES)
            step(PAIRS - 2, 0, 1, [])
            step(PAIRS - 1, 1, 0, [])
            step(PAIRS - 1, 1, 1, [], last=True)
            normalise(4 * PAIRS - 1)
            residual(4 * PAIRS - 1, 4 * PAIRS - 1)
            after(4 * PAIRS - 2, 4 * PAIRS - 3)
            after(4 * PAIRS - 1, 4 * PAIRS - 1)
            next_ln[1](6)
            dve_columns(v, LN[2 * a + 1], 1, slice(TILES - 4, TILES))
            for stage in next_ln:
                stage(7)
            v.wait_ge(LN[2 * a + 1].logit, 8)
            nc.vector.tensor_copy(lg[:], ps[:, 5, 0:TILES * EXPERTS]).then_inc(LN[2 * a + 1].logit_out, 1)

        def dve_threshold(v, s):
            n = [0]

            def link(m):
                n[0] += 1
                m.then_inc(s.step, 1)
                v.wait_ge(s.step, n[0])

            neg, sgn, need, kth, reached = (tv[:, k:k + 1] for k in range(5))
            digits = tv[:, 5:8]
            have, got = ti[:, 0:1], ti[:, 1:2]
            cand, place, nxt = ti[:, 2:5], ti[:, 5:8], ti[:, 8:11]
            total = NT * EXPERTS
            nc.vector.tensor_scalar(junk[0], lg[:], 0.0, 0.0, ALU.is_lt, ALU.add, accum_out=cnt[:, 0:1]).then_inc(s.cnt, 1)
            v.wait_ge(s.tot, 1)
            link(nc.vector.tensor_scalar(neg, ps[:, 6, 0:1], float(GATED), None, ALU.is_ge))
            link(nc.vector.tensor_scalar(sgn, neg, -2.0, 1.0, ALU.mult, ALU.add))
            link(nc.vector.tensor_scalar(need, neg, float(2 * GATED - total - 1), float(total - GATED + 1),
                                         ALU.mult, ALU.add))
            link(nc.vector.tensor_scalar(zt, lg[:], sgn, None, ALU.mult))
            link(nc.vector.memset(have, 0))
            for k in range(3):
                link(nc.vector.memset(tv[:, 5 + k:6 + k], float((k + 1) * 2 ** 29)))
            link(nc.vector.tensor_copy(cand, digits))
            base = n[0]
            with v.Fori(0, 5) as i:
                for r in (3 * i, 3 * i + 1, 3 * i + 2):
                    v.wait_ge(s.step, base + 7 * r)
                    for k in range(3):
                        nc.vector.tensor_scalar(junk[k], zt, cand[:, k:k + 1].bitcast(F32), 0.0, ALU.is_ge, ALU.add,
                                                accum_out=cnt[:, k:k + 1]).then_inc(s.cnt, 1)
                    nc.vector.tensor_scalar(place, digits, 0.25, None, ALU.mult).then_inc(s.step, 1)
                    v.wait_ge(s.step, base + 7 * r + 1)
                    nc.vector.tensor_tensor(nxt, place, have.broadcast_to([P, 3]), ALU.bitwise_or).then_inc(s.step, 1)
                    v.wait_ge(s.tot, r + 2)
                    nc.vector.tensor_scalar(flags[:], ps[:, 6, 0:3], need, 0.0, ALU.is_ge, ALU.add, accum_out=reached)\
                      .then_inc(s.step, 1)
                    v.wait_ge(s.step, base + 7 * r + 3)
                    nc.vector.tensor_scalar(got, reached, digits[:, 0:1], None, ALU.mult).then_inc(s.step, 1)
                    v.wait_ge(s.step, base + 7 * r + 4)
                    nc.vector.tensor_tensor(cand, nxt, got.broadcast_to([P, 3]), ALU.bitwise_or).then_inc(s.step, 1)
                    nc.vector.tensor_tensor(have, have, got, ALU.bitwise_or).then_inc(s.step, 1)
                    nc.vector.tensor_scalar(digits, digits, 0.25, None, ALU.mult).then_inc(s.step, 1)
            n[0] = base + 7 * 15
            v.wait_ge(s.step, n[0])
            nc.vector.tensor_scalar(junk[0], zt, cand[:, 1:2].bitcast(F32), 0.0, ALU.is_ge, ALU.add,
                                    accum_out=cnt[:, 0:1]).then_inc(s.cnt, 1)
            v.wait_ge(s.tot, 17)
            link(nc.vector.tensor_scalar(got, ps[:, 6, 0:1], need, None, ALU.is_ge))
            link(nc.vector.tensor_tensor(have, have, got, ALU.bitwise_or))
            link(nc.vector.tensor_scalar(kth, have.bitcast(F32), sgn, None, ALU.mult))
            nc.vector.scalar_tensor_tensor(out=lg[:], in0=lg[:], scalar=kth, in1=lg[:], op0=ALU.is_ge, op1=ALU.mult)\
              .then_inc(s.gate, 1)
            v.wait_ge(s.gate, 1)

        def dve_ffn(v, s, ln):
            def split(i, e):
                n = EXPERTS * i + e
                hi, lo = ((hh, hl), (hh2, hl2))[e % 2]
                v.wait_ge(s.mm2, ONE + n - 1)
                for c in range(HC):
                    v.wait_ge(s.high, HC * n + c + 1)
                    w = slice(c * 512, c * 512 + 512)
                    nc.vector.tensor_tensor(lo[:, w], h32[:, w], hi[:, w], ALU.subtract).then_inc(s.low, 1)

            def gated(i, e):
                v.wait_ge(s.mm2, ONE + EXPERTS * i + e + 1)
                v.wait_ge(s.gated, ONE + EXPERTS * i + e)
                if e == 0:
                    v.wait_ge(s.gst, i + 1)
                if e == 3:
                    v.wait_ge(s.b2_used, ONE + i + 1)
                for t in range(4):
                    xc = xs[:, bass.ds(i * 512 + t * P, P)]
                    m = nc.vector.scalar_tensor_tensor(out=xc, in0=ps[:, 4 + e % 2, t * P:t * P + P],
                                                       scalar=gst[:, t * EXPERTS + e:t * EXPERTS + e + 1], in1=xc,
                                                       op0=ALU.mult, op1=ALU.add)
                m.then_inc(s.gated, 1)
                if e == EXPERTS - 1 and ln:
                    v.wait_ge(s.gated, ONE + EXPERTS * (i + 1))
                    for t in range(4):
                        statistics(4 * i + t, ln)

            def tokens(i, last):
                v.wait_ge(s.gated, ONE + EXPERTS * i)
                nc.vector.tensor_copy(gst, lg[:, bass.ds(i * 32, 32)]).then_inc(s.gst, 1)
                for e in range(1, EXPERTS + 1 - last):
                    split(i + e // EXPERTS, e % EXPERTS)
                    if e == 2:
                        v.wait_ge(s.gT, i + 1)
                        nc.vector.tensor_copy(gtt, ps[0:EXPERTS, 6, :]).then_inc(s.gTs, 1)
                    gated(i, e - 1)
                    if e == 3:
                        v.wait_ge(s.b2, i + 1)
                        v.wait_ge(s.gated, ONE + EXPERTS * i + 3)
                        xc = xs[:, bass.ds(i * 512, 512)]
                        nc.vector.tensor_tensor(xc, xc, ps[:, 7, :], ALU.add).then_inc(s.b2_used, 1)

            split(0, 0)
            with v.Fori(0, BLOCKS - 1) as i:
                tokens(i, False)
            tokens(BLOCKS - 1, True)
            gated(BLOCKS - 1, EXPERTS - 1)

        @block.vector
        def _(v):
            dve_setup(v)
            dve_attn(v, 0)
            v.wait_ge(LN[1].logit_out, 1)
            dve_threshold(v, TH[0])
            dve_ffn(v, FF[0], LN[2])
            v.wait_ge(FF[0].gated, ONE + BLOCKS * EXPERTS)
            dve_attn(v, 1)
            v.wait_ge(LN[3].logit_out, 1)
            dve_threshold(v, TH[1])
            dve_ffn(v, FF[1], None)

        @block.gpsimd
        def _(pool):
            nc.gpsimd.memset(zero32[:], 0.0).then_inc(su.ready, 1)
            nc.gpsimd.memset(zero16[:], 0.0).then_inc(su.ready, 1)
            for a in range(2):
                s = AT[a]
                if a:
                    pool.wait_ge(FF[0].mm2, ONE + BLOCKS * EXPERTS)
                nc.gpsimd.memset(share[:], 0.0).then_inc(su.ready, 1)
                pool.wait_ge(su.ready, 3 + a)

                def blocks(p, par):
                    since(pool, s.s2, 32 * (p - 1))
                    pool.wait_ge(s.split, 8 * p + SLOTS)
                    for qh in range(2):
                        for g in range(G):
                            rows = slice(32 * g, 32 * g + 32)
                            o = qh * QCOLS + g * QCOLS // G
                            for b in range(NB):
                                src = qs[rows, :].rearrange("p (s b h q) -> p s b h q", s=SLOTS, b=NB, h=2)[:, :, b, qh, :]
                                dst = qm[par][rows, o + b * SLOTS * QH:o + (b + 1) * SLOTS * QH].rearrange(
                                    "p (s q) -> p s q", s=SLOTS)
                                m = nc.gpsimd.tensor_tensor(
                                    dst, src, zero16[rows, :].unsqueeze(2).broadcast_to([32, SLOTS, QH]), ALU.add)
                            if g == 0:
                                nc.gpsimd.memset(qm[par][rows, o + QCOLS // G:o + QCOLS], 0.0)
                            m.then_inc(s.qm, 1)

                blocks(0, 0)
                pool.wait_ge(LN[2 * a].normed, 8)
                pool.wait_ge(LN[2 * a].normed2, 8)
                pool.wait_ge(s.qm, 8)
                for n in range(4):
                    xc = xs[:, 1024 * n:1024 * n + 1024].rearrange("p (t c) -> p t c", c=P)
                    nc.gpsimd.tensor_tensor(xc, xc, bp[a][:].unsqueeze(1).broadcast_to([P, 8, P]), ALU.add)\
                      .then_inc(s.bias, 1)
                pool.wait_ge(s.bias, 4)
                blocks(1, 1)
                with pool.Fori(1, PAIRS // 2) as i:
                    blocks(2 * i, 0)
                    blocks(2 * i + 1, 1)
                pool.wait_ge(FF[a].w_high, 2)
                nc.gpsimd.tensor_tensor(w1l, raw1, w1h, ALU.subtract).then_inc(FF[a].w_low, 1)
                nc.gpsimd.tensor_tensor(w2l, raw2, w2h, ALU.subtract).then_inc(FF[a].w_low, 1)
                f = FF[a]
                with pool.Fori(0, BLOCKS) as i:
                    for e in range(EXPERTS):
                        n = EXPERTS * i + e
                        hi = (hh, hh2)[e % 2]
                        pool.wait_ge(f.mm2, ONE + n - 1)
                        for c in range(HC):
                            w = slice(c * 512, c * 512 + 512)
                            pool.wait_ge(f.gelu, ONE + HC * n + c + 1)
                            nc.gpsimd.tensor_tensor(hi[:, w], h32[:, w], zero32[:].broadcast_to([P, 512]), ALU.add)\
                              .then_inc(f.high, 1)


def kernel(**inputs):
    import numpy as np
    import concourse.bacc as bacc
    from concourse.bass_utils import run_bass_kernel_spmd as run

    g = {k: np.asarray(v) for k, v in inputs.items()}

    def heads_rows(w):
        n = w.shape[1]
        r = w.reshape(SLOTS, G, DH, n)
        z = np.zeros((SLOTS, G, DH, n), w.dtype)
        return np.concatenate([r, r, r, z], axis=2).reshape(SLOTS, P, n).transpose(1, 0, 2)

    def weights(pre, last):
        q, k, v, p = (g[f"{pre}_W{n}"] for n in ("q", "k", "v", last))
        blocks = [heads_rows(q), heads_rows(k), v[:, None, :], p[:, None, :]]
        return np.ascontiguousarray(np.concatenate(blocks, axis=1).reshape(P, BLK * P))

    def qk_bias(pre):
        q = heads_rows(g[f"{pre}_bq"][:, None])[:, :, 0]
        k = heads_rows(g[f"{pre}_bk"][:, None])[:, :, 0].copy()
        k[MROW, :] = MSCALE
        return np.ascontiguousarray(np.concatenate([q, k], axis=1))

    row = np.arange(P) % 32
    masks = np.stack([-((row >= 16) & (row < 24)).astype(np.float32), -((row >= 8) & (row < 16)).astype(np.float32)], 1)
    rel = g["L0_attn_b_rel_emb"]
    rel = rel[np.clip(np.arange(REL) - (T - 1), -REL_MAX, REL_MAX) + REL_MAX].T
    rel = np.tile(np.concatenate([rel, rel, rel, np.zeros_like(rel)], axis=0), (G, 1))
    arrays = {
        "x": g["L0_attn_a_x"].reshape(TILES, P, D).transpose(1, 0, 2).reshape(P, NT),
        "wa": weights("L0_attn_a", "p"), "wb": weights("L0_attn_b", "o"),
        "bias_a": qk_bias("L0_attn_a"), "bias_b": qk_bias("L0_attn_b"),
        "bv_a": np.tile(g["L0_attn_a_bv"][None, :], (P, 1)), "bv_b": np.tile(g["L0_attn_b_bv"][None, :], (P, 1)),
        "bp_a": np.tile(g["L0_attn_a_bp"][None, :], (P, 1)), "bp_b": np.tile(g["L0_attn_b_bo"][None, :], (P, 1)),
        "rel": rel, "masks": masks, "ident": np.eye(P, dtype=np.float32),
        "gate": g["L0_ffn_gate_weight"].T,
        "w1": g["L0_ffn_w1"].reshape(EXPERTS * HID, D).T,
        "b1": g["L0_ffn_b1"].reshape(EXPERTS * HC, P).T,
        "w2": g["L0_ffn_w2"].transpose(2, 0, 1).reshape(HC, P, EXPERTS, D).transpose(1, 2, 0, 3).reshape(P, EXPERTS * HID),
        "b2": g["L0_ffn_b2"],
    }
    nc = bacc.Bacc("TRN2", target_bir_lowering=False, num_devices=1)
    args = []
    for name in list(arrays):
        arrays[name] = np.ascontiguousarray(arrays[name])
        args.append(nc.dram_tensor(name, arrays[name].shape, F32, kind="ExternalInput").ap())
    args.append(nc.dram_tensor("out", (P, NT), F32, kind="ExternalOutput").ap())
    network(nc, *args)
    r = run(nc, [arrays], core_ids=[0])
    y = r.results[0]["out"]
    return np.ascontiguousarray(y.reshape(P, TILES, D).transpose(1, 0, 2).reshape(B, T, D))
```
